# Optimizing a Trainium2 kernel written in Bass

```python
import numpy as np
import jax
import jax.numpy as jnp

def _softmax(x, axis=-1):
    return jax.nn.softmax(x, axis=axis)

def _gelu(x):
    return jax.nn.gelu(x, approximate=True)

def _silu(x):
    return jax.nn.silu(x)

def _sigmoid(x):
    return jax.nn.sigmoid(x)

def _layernorm(x, axis=-1, eps=1e-05):
    m = jnp.mean(x, axis=axis, keepdims=True)
    v = jnp.var(x, axis=axis, keepdims=True)
    return (x - m) / jnp.sqrt(v + eps)

def _scatter_add(tgt, idx, src, axis=0):
    return tgt.at[idx].add(src)

def _segment_sum(src, seg, n):
    return jax.ops.segment_sum(src, seg, n)
kernel_name = 'mk_flamingo_gated_d1_seqx_r8_08dbc1'

def setup_inputs(seed: int=0):
    np.random.seed(seed)
    _w = jnp.asarray

    def _rec_inputs():
        import jax
        import jax.numpy as jnp
        _rk = jax.random.key(seed)
        x = 0.0001212 + 1 * jax.random.normal(jax.random.fold_in(_rk, 1), (8, 128, 512), jnp.float32)
        _lenS = 128 - jax.random.randint(jax.random.fold_in(_rk, 7), (8,), 0, max(1, 128 // 4) + 1, jnp.int32)
        _lenS2 = 128 - jax.random.randint(jax.random.fold_in(_rk, 8), (8,), 0, max(1, 128 // 4) + 1, jnp.int32)
        _ctx_4096P = jax.random.normal(jax.random.fold_in(_rk, 11), (8, 16, 512), jnp.float32)
        _ctx_4096c = jax.random.dirichlet(jax.random.fold_in(_rk, 511), 0.3 * jnp.ones((16,), jnp.float32), (8, 128))
        _ctx_4096t = jnp.einsum('bsk,bkd->bsd', _ctx_4096c, _ctx_4096P)
        _ctx_4096t = _ctx_4096t * jax.lax.rsqrt(jnp.mean(jnp.square(_ctx_4096t)) + 1e-12) * 0.953939
        ctx_4096 = -0.000125008 + 0.999885 * (_ctx_4096t + 0.3 * jax.random.normal(jax.random.fold_in(_rk, 611), (8, 128, 512), jnp.float32))
        _g = jax.random.normal(jax.random.fold_in(_rk, 9001), (2, 1), jnp.float32)
        _g = jnp.sign(_g) * jnp.maximum(jnp.abs(_g), 1.0) + (_g == 0) * 1.0
        g_xattn = _g[0]
        g_ffn = _g[1]
        return (x, ctx_4096, g_xattn, g_ffn)
    x, ctx_4096, g_xattn, g_ffn = _rec_inputs()

    def _L0_xattn_setup():
        import jax, jax.numpy as jnp
        import numpy as np
        N, C, S = (16, 64, 512)
        rng = jax.random.key(seed)
        k1, k2, k3 = jax.random.split(rng, 3)
        return {'key': jax.random.normal(k1, (N, C, S), dtype=jnp.float32), 'value': jax.random.normal(k2, (N, C, S), dtype=jnp.float32), 'query': jax.random.normal(k3, (N, C, S), dtype=jnp.float32)}
    _L0_xattn_all = _L0_xattn_setup()
    _L0_xattn_in = {k: v for k, v in _L0_xattn_all.items() if k in ()}
    del _L0_xattn_all

    def _L0_ffn_setup():
        import jax, jax.numpy as jnp
        import numpy as np
        HID, INT, LAT, NE, K = (512, 1024, 256, 8, 2)
        LN_EPS = 1e-05

        def _layernorm(x, gamma, beta):
            mu = jnp.mean(x, axis=-1, keepdims=True)
            var = jnp.var(x, axis=-1, keepdims=True)
            return (x - mu) * jax.lax.rsqrt(var + LN_EPS) * gamma + beta
        key = jax.random.key(seed)
        ks = jax.random.split(key, 8)
        s = lambda d: 1.0 / np.sqrt(d)
        return {'hidden_states': jax.random.normal(ks[0], (4, 256, HID), jnp.float32), 'gate_w': jax.random.normal(ks[1], (HID, NE), jnp.float32) * s(HID), 'up_w': jax.random.normal(ks[2], (HID, INT), jnp.float32) * s(HID), 'down_w': jax.random.normal(ks[3], (INT, HID), jnp.float32) * s(INT), 'fc1_w': jax.random.normal(ks[4], (HID, LAT), jnp.float32) * s(HID), 'fc2_w': jax.random.normal(ks[5], (LAT, HID), jnp.float32) * s(LAT), 'expert_w': jax.random.normal(ks[6], (LAT, LAT), jnp.float32), 'ln_gamma': jnp.ones((HID,), jnp.float32), 'ln_beta': jnp.zeros((HID,), jnp.float32)}
    _L0_ffn_all = _L0_ffn_setup()
    _L0_ffn_in = {k: v for k, v in _L0_ffn_all.items() if k in ('gate_w', 'up_w', 'down_w', 'fc1_w', 'fc2_w', 'expert_w', 'ln_gamma', 'ln_beta')}
    del _L0_ffn_all
    return {'x': x, 'ctx_4096': ctx_4096, 'g_xattn': g_xattn, 'g_ffn': g_ffn, 'L0_ffn_gate_w': _L0_ffn_in['gate_w'], 'L0_ffn_up_w': _L0_ffn_in['up_w'], 'L0_ffn_down_w': _L0_ffn_in['down_w'], 'L0_ffn_fc1_w': _L0_ffn_in['fc1_w'], 'L0_ffn_fc2_w': _L0_ffn_in['fc2_w'], 'L0_ffn_expert_w': _L0_ffn_in['expert_w'], 'L0_ffn_ln_gamma': _L0_ffn_in['ln_gamma'], 'L0_ffn_ln_beta': _L0_ffn_in['ln_beta']}

def reference(x, ctx_4096, g_xattn, g_ffn, L0_ffn_gate_w, L0_ffn_up_w, L0_ffn_down_w, L0_ffn_fc1_w, L0_ffn_fc2_w, L0_ffn_expert_w, L0_ffn_ln_gamma, L0_ffn_ln_beta):
    import jax
    import jax.numpy as jnp

    def _L0_xattn_ref(key, value, query):
        import jax, jax.numpy as jnp
        import numpy as np
        N, C, S = (16, 64, 512)
        KC = key.shape[1]
        sim = jnp.einsum('ncs,nds->ncd', key, query) * KC ** (-0.5)
        sim = jax.nn.softmax(sim, axis=1)
        context = jnp.einsum('ncd,nds->ncs', sim, value)
        return context

    def _L0_ffn_ref(hidden_states, gate_w, up_w, down_w, fc1_w, fc2_w, expert_w, ln_gamma, ln_beta):
        import jax, jax.numpy as jnp
        import numpy as np
        HID, INT, LAT, NE, K = (512, 1024, 256, 8, 2)
        LN_EPS = 1e-05

        def _layernorm(x, gamma, beta):
            mu = jnp.mean(x, axis=-1, keepdims=True)
            var = jnp.var(x, axis=-1, keepdims=True)
            return (x - mu) * jax.lax.rsqrt(var + LN_EPS) * gamma + beta
        logits = jnp.einsum('bsh,he->bse', hidden_states, gate_w)
        routing_weights, selected_experts = jax.lax.top_k(logits, K)
        h = jax.nn.relu(jnp.einsum('bsh,hi->bsi', hidden_states, up_w)) ** 2
        shared_out = jnp.einsum('bsi,ih->bsh', h, down_w)
        x_latent = jnp.einsum('bsh,hl->bsl', hidden_states, fc1_w)
        expert_out = jnp.einsum('bsl,lm->bsm', x_latent, expert_w)
        moe_out = expert_out * jnp.sum(routing_weights, axis=-1, keepdims=True)
        routed_out = jnp.einsum('bsl,lh->bsh', moe_out, fc2_w)
        return _layernorm(shared_out + routed_out, ln_gamma, ln_beta)
    x = x + jnp.tanh(g_xattn[0]) * _L0_xattn_ref(ctx_4096, ctx_4096, _layernorm(x, axis=-1))
    x = x + jnp.tanh(g_ffn[0]) * _L0_ffn_ref(_layernorm(x, axis=-1), L0_ffn_gate_w, L0_ffn_up_w, L0_ffn_down_w, L0_ffn_fc1_w, L0_ffn_fc2_w, L0_ffn_expert_w, L0_ffn_ln_gamma, L0_ffn_ln_beta)
    return x

_drawn_inputs = setup_inputs


def setup_inputs(seed=0):
    import zlib

    import numpy as np

    out = dict(_drawn_inputs(seed))
    spreads = {'L0_ffn_ln_gamma': (1.0, 0.2), 'L0_ffn_ln_beta': (0.0, 0.1)}
    factors = {}
    for name, (base, spread) in spreads.items():
        noise = np.random.default_rng([zlib.crc32(name.encode()), seed]).standard_normal(out[name].shape)
        drawn = base * np.exp(spread * noise) if base else spread * noise
        out[name] = jnp.asarray(drawn.astype(out[name].dtype))
    for name, factor in factors.items():
        out[name] = (out[name] * factor).astype(out[name].dtype)
    return out
```

```python
from contextlib import ExitStack

import concourse.bass as bass
from concourse import mybir

F32 = mybir.dt.float32
F32R = mybir.dt.float32r
ALU = mybir.AluOpType
ACT = mybir.ActivationFunctionType
AX = mybir.AxisListType

P = 128
PAIR = 2
EPS = 1e-5
RING = 4


def flamingo_block(nc, x, ctx_in, g_xattn, g_ffn, gate_w, up_w, down_w, fc1_w, fc2_w, expert_w,
                   ln_gamma, ln_beta, out):
    BATCH, TOK, HID = x.shape
    INNER = up_w.shape[1]
    LAT = fc1_w.shape[1]
    NE = gate_w.shape[1]
    KH = HID // P
    KI = INNER // P
    KL = LAT // P
    GROUPS = BATCH // PAIR
    GT = PAIR * TOK
    UPS = KI // PAIR
    SCALE = float(TOK) ** -0.5
    assert TOK == P and HID == 512 and GT * PAIR == 512 and NE == 8

    def nth(n, b):
        return PAIR * n + b + 1

    def is_first(g):
        return isinstance(g, int) and g == 0

    stack = ExitStack()
    with stack:
        def sb(name, shape, dt=F32):
            return stack.enter_context(nc.sbuf_tensor(name, shape, dt))

        def bank(name):
            return stack.enter_context(nc.psum_tensor(name, [P, 512], F32))

        def sem(name):
            return stack.enter_context(nc.semaphore(name))

        up_bank = [bank("up_bank0"), bank("up_bank1")]
        down_bank = [bank("down_bank0"), bank("down_bank1")]
        routed_bank = bank("routed_bank")
        ctx_bank = bank("ctx_bank")
        tok_bank = bank("tok_bank")
        small_bank = bank("small_bank")

        xs = sb("xs", [P, BATCH, HID])
        ctx = sb("ctx", [P, PAIR, HID])
        v_hi = sb("v_hi", [P, PAIR, HID], F32R)
        v_lo = sb("v_lo", [P, PAIR, HID], F32R)
        ctxT_hi = sb("ctxT_hi", [P, PAIR, KH, TOK], F32R)
        ctxT_lo = sb("ctxT_lo", [P, PAIR, KH, TOK], F32R)
        qT_hi = sb("qT_hi", [P, PAIR, KH, TOK], F32R)
        qT_lo = sb("qT_lo", [P, PAIR, KH, TOK], F32R)
        normed = sb("normed", [P, PAIR, HID])
        hT_hi = sb("hT_hi", [P, KH, GT], F32R)
        hT_lo = sb("hT_lo", [P, KH, GT], F32R)
        act2 = sb("act2", [P, 2, PAIR, GT])
        act2_hi = sb("act2_hi", [P, KI, GT], F32R)
        act2_lo = sb("act2_lo", [P, KI, GT], F32R)
        y = sb("y", [P, PAIR, HID])
        probs = sb("probs", [P, PAIR, TOK])
        probs_hi = sb("probs_hi", [P, PAIR, TOK], F32R)
        probs_lo = sb("probs_lo", [P, PAIR, TOK], F32R)

        raw = sb("raw", [P, RING, 1024])
        up_hi = sb("up_hi", [P, UPS, KH, PAIR * P], F32R)
        up_lo = sb("up_lo", [P, UPS, KH, PAIR * P], F32R)
        down_hi = sb("down_hi", [P, KI, HID], F32R)
        down_lo = sb("down_lo", [P, KI, HID], F32R)
        W_hi = sb("W_hi", [P, KH, HID], F32R)
        W_lo = sb("W_lo", [P, KH, HID], F32R)
        lat_hi = sb("lat_hi", [P, KL, HID], F32R)
        lat_lo = sb("lat_lo", [P, KL, HID], F32R)
        expert_hi = sb("expert_hi", [P, KL, LAT], F32R)
        expert_lo = sb("expert_lo", [P, KL, LAT], F32R)
        fc2_hi = sb("fc2_hi", [P, KL, HID], F32R)
        fc2_lo = sb("fc2_lo", [P, KL, HID], F32R)
        gate = sb("gate", [P, KH, NE])
        gate_hl = sb("gate_hl", [P, KH, 2, NE], F32R)
        gamma = sb("gamma", [P, HID])
        beta = sb("beta", [P, HID])
        gates = sb("gates", [P, 2])
        ident = sb("ident", [P, P])
        neg_half = sb("neg_half", [P, 1])

        LNS = ("x", "x1", "y")
        stats = {k: sb(f"stats_{k}", [P, PAIR, 6]) for k in LNS}
        moments = {k: sb(f"moments_{k}", [P, PAIR, 2]) for k in LNS}
        rstd = {k: sb(f"rstd_{k}", [P, PAIR, 1]) for k in LNS}
        neg_max = sb("neg_max", [P, PAIR, 1])
        exp_sum = sb("exp_sum", [P, PAIR, 1])
        exp_inv = sb("exp_inv", [P, PAIR, 1])
        row_max = sb("row_max", [P, PAIR, 1])
        logits = sb("logits", [P, PAIR, NE])
        top8 = sb("top8", [P, PAIR, 8])
        route = sb("route", [P, PAIR])

        x_loaded = [sem(f"x_loaded{b}") for b in range(PAIR)]
        ctx_loaded = [sem(f"ctx_loaded{b}") for b in range(PAIR)]
        gates_loaded = sem("gates_loaded")
        gate_loaded = sem("gate_loaded")
        affine_loaded = sem("affine_loaded")
        PIECES = ["fc1", "expert", "fc2"] + [f"up{j}" for j in range(UPS)] + [f"down{j}" for j in range(UPS)]
        raw_loaded = {k: sem(f"{k}_loaded") for k in PIECES}
        out_stored = sem("out_stored")
        waits_passed = sem("waits_passed")
        ident_zeroed = sem("ident_zeroed")
        ident_ready = sem("ident_ready")
        half_ready = sem("half_ready")
        tanh_ready = sem("tanh_ready")
        affine_ready = sem("affine_ready")
        hi_ready = {k: sem(f"{k}_hi_ready") for k in PIECES[1:]}
        lo_ready = {k: sem(f"{k}_lo_ready") for k in PIECES[1:]}
        gate_hi_ready = sem("gate_hi_ready")
        gate_lo_ready = sem("gate_lo_ready")
        fc1T_made = sem("fc1T_made")
        fc1T_hi_ready = sem("fc1T_hi_ready")
        fc1T_lo_ready = sem("fc1T_lo_ready")
        latW_made = sem("latW_made")
        latW_hi_ready = sem("latW_hi_ready")
        latW_lo_ready = sem("latW_lo_ready")
        W_made = sem("W_made")
        W_hi_ready = sem("W_hi_ready")
        W_lo_ready = sem("W_lo_ready")
        stats_ready = {k: sem(f"stats_{k}_ready") for k in LNS}
        moments_ready = {k: sem(f"moments_{k}_ready") for k in LNS}
        var_ready = {k: sem(f"var_{k}_ready") for k in LNS}
        rstd_ready = {k: sem(f"rstd_{k}_ready") for k in LNS}
        q_ready = sem("q_ready")
        v_hi_ready = sem("v_hi_ready")
        v_lo_ready = sem("v_lo_ready")
        ctxT_made = sem("ctxT_made")
        ctxT_hi_ready = sem("ctxT_hi_ready")
        ctxT_lo_ready = sem("ctxT_lo_ready")
        qT_made = sem("qT_made")
        qT_hi_ready = sem("qT_hi_ready")
        qT_lo_ready = sem("qT_lo_ready")
        scores_made = sem("scores_made")
        row_max_ready = sem("row_max_ready")
        neg_max_ready = sem("neg_max_ready")
        exp_ready = sem("exp_ready")
        exp_inv_ready = sem("exp_inv_ready")
        probs_ready = sem("probs_ready")
        probs_hi_ready = sem("probs_hi_ready")
        probs_lo_ready = sem("probs_lo_ready")
        attended = sem("attended")
        x1_ready = sem("x1_ready")
        h_ready = sem("h_ready")
        hT_made = sem("hT_made")
        hT_hi_ready = sem("hT_hi_ready")
        hT_lo_ready = sem("hT_lo_ready")
        up_made = sem("up_made")
        relu_ready = sem("relu_ready")
        square_ready = sem("square_ready")
        act2_hi_ready = sem("act2_hi_ready")
        act2_lo_ready = sem("act2_lo_ready")
        logits_made = sem("logits_made")
        logits_ready = sem("logits_ready")
        top_ready = sem("top_ready")
        route_ready = sem("route_ready")
        routed_made = sem("routed_made")
        scaled_ready = sem("scaled_ready")
        down_made = sem("down_made")
        y_ready = sem("y_ready")
        x1_beta_ready = sem("x1_beta_ready")
        y_gamma_ready = sem("y_gamma_ready")
        out_ready = sem("out_ready")

        def flat(t, *at):
            v = t[(slice(None),) + at]
            return v.rearrange("p a b -> p (a b)") if len(v.shape) == 3 else v

        piece = {
            "fc1": (fc1_w.rearrange("(k p) l -> p k l", p=P), raw[:, 0, 0:KH * LAT], None, None),
            "expert": (expert_w.rearrange("(k p) l -> p k l", p=P), raw[:, 1, 0:KL * LAT],
                       flat(expert_hi), flat(expert_lo)),
            "fc2": (fc2_w.rearrange("(k p) n -> p k n", p=P), raw[:, 2, 0:KL * HID],
                    flat(fc2_hi), flat(fc2_lo)),
        }
        for j in range(UPS):
            piece[f"up{j}"] = (up_w.rearrange("(k p) i -> p k i", p=P)[:, :, j * PAIR * P:(j + 1) * PAIR * P],
                               raw[:, (3 + j) % RING, 0:KH * PAIR * P], flat(up_hi, j), flat(up_lo, j))
            piece[f"down{j}"] = (down_w.rearrange("(k p) n -> p k n", p=P)[:, PAIR * j:PAIR * (j + 1), :],
                                 raw[:, (3 + UPS + j) % RING, 0:PAIR * HID],
                                 flat(down_hi, slice(PAIR * j, PAIR * (j + 1))),
                                 flat(down_lo, slice(PAIR * j, PAIR * (j + 1))))

        def f32(ap):
            return ap.bitcast(F32)

        def tokens(b):
            return slice(b * TOK, (b + 1) * TOK)

        def wait_apart(engine, on, value):
            engine.wait_ge(on, value)
            engine.sem_inc(waits_passed, 1)

        block = stack.enter_context(nc.Block())

        @block.sync
        def _(sp):
            def load_x(n, b):
                if not is_first(n):
                    sp.wait_ge(stats_ready["x"], nth(n, b) - PAIR)
                sp.dma_start(xs[:, PAIR * n + b, :], x[PAIR * n + b]).then_inc(x_loaded[b], 16)

            def load_ctx(n, b):
                if not is_first(n):
                    sp.wait_ge(v_hi_ready, nth(n, b) - PAIR)
                    sp.wait_ge(v_lo_ready, nth(n, b) - PAIR)
                    sp.wait_ge(ctxT_made, nth(n, b) - PAIR)
                sp.dma_start(ctx[:, b, :], ctx_in[PAIR * n + b]).then_inc(ctx_loaded[b], 16)

            def load_piece(k):
                at = PIECES.index(k)
                if at >= RING:
                    before = PIECES[at - RING]
                    if before == "fc1":
                        sp.wait_ge(fc1T_made, KL)
                    else:
                        sp.wait_ge(hi_ready[before], 1)
                        sp.wait_ge(lo_ready[before], 1)
                src, dst, _, _ = piece[k]
                sp.dma_start(dst.rearrange("p (k n) -> p k n", k=src.shape[1]), src).then_inc(raw_loaded[k], 16)

            def store(g, b):
                sp.wait_ge(out_ready, nth(g, b))
                sp.dma_start(out[PAIR * g + b], xs[:, PAIR * g + b, :]).then_inc(out_stored, 16)

            load_x(0, 0)
            load_ctx(0, 0)
            load_x(0, 1)
            load_ctx(0, 1)
            for g_at, g_in in enumerate((g_xattn, g_ffn)):
                sp.dma_start(gates[:, g_at:g_at + 1], g_in.rearrange("(a d) -> a d", a=1).to_broadcast([P, 1])
                             ).then_inc(gates_loaded, 16)
            for k in PIECES[:5]:
                load_piece(k)
            sp.dma_start(gate[:], gate_w.rearrange("(k p) e -> p k e", p=P)).then_inc(gate_loaded, 16)
            for k in PIECES[5:7]:
                load_piece(k)
            load_x(1, 0)
            load_ctx(1, 0)
            load_x(1, 1)
            load_ctx(1, 1)
            for k in PIECES[7:]:
                load_piece(k)
            for t, src in ((gamma, ln_gamma), (beta, ln_beta)):
                sp.dma_start(t[:], src.rearrange("(a d) -> a d", a=1).to_broadcast([P, HID])
                             ).then_inc(affine_loaded, 16)
            with sp.Fori(0, GROUPS - 2) as g:
                for b in range(PAIR):
                    sp.wait_ge(stats_ready["x"], PAIR * g + b + 1 + PAIR)
                    sp.dma_start(xs[:, PAIR * g + 2 * PAIR + b, :], x[PAIR * g + 2 * PAIR + b]
                                 ).then_inc(x_loaded[b], 16)
                    load_ctx(g + 2, b)
                for b in range(PAIR):
                    store(g, b)
            for g in range(GROUPS - 2, GROUPS):
                for b in range(PAIR):
                    store(g, b)
            sp.wait_ge(out_stored, 16 * BATCH)

        @block.tensor
        def _(pe):
            def product(to, parts, first, last):
                mm = None
                for at, (a_hi, a_lo, b_hi, b_lo) in enumerate(parts):
                    begins, ends = first and at == 0, last and at == len(parts) - 1
                    pe.matmul(to, a_hi, b_hi, start=begins, stop=False)
                    pe.matmul(to, a_hi, b_lo, start=False, stop=False)
                    mm = pe.matmul(to, a_lo, b_hi, start=False, stop=ends)
                return mm

            def transposed(to, src, made):
                for k in range(KH):
                    mm = pe.transpose(to[:, k * P:(k + 1) * P], src[:, k * P:(k + 1) * P], ident[:])
                mm.then_inc(made, 1)

            def transpose_ctx(n, b):
                pe.wait_ge(ctx_loaded[b], 16 * (n + 1))
                if b:
                    pe.wait_ge(ctxT_lo_ready, nth(n, b) - 1)
                elif not is_first(n):
                    pe.wait_ge(x1_ready, nth(n, b) - 1)
                transposed(ctx_bank, ctx[:, b, :], ctxT_made)

            def transpose_q(n, b):
                pe.wait_ge(q_ready, nth(n, b))
                if b:
                    pe.wait_ge(qT_lo_ready, nth(n, b) - 1)
                elif not is_first(n):
                    pe.wait_ge(hT_lo_ready, nth(n, b) - 1)
                transposed(tok_bank, normed[:, b, :], qT_made)

            def scores(n, b):
                pe.wait_ge(qT_lo_ready, nth(n, b))
                pe.wait_ge(ctxT_lo_ready, nth(n, b))
                if b == 0 and not is_first(n):
                    pe.wait_ge(exp_ready, nth(n, b) - 1)
                if b == 1 and is_first(n):
                    pe.wait_ge(exp_ready, nth(n, b) - 1)
                if b == 1 and not is_first(n):
                    pe.wait_ge(logits_ready, n)
                product(small_bank[:, 0:TOK],
                        [(qT_hi[:, b, k, :], qT_lo[:, b, k, :], ctxT_hi[:, b, k, :], ctxT_lo[:, b, k, :])
                         for k in range(KH)], True, True).then_inc(scores_made, 1)

            def attend(n, b):
                pe.wait_ge(probs_lo_ready, nth(n, b))
                pe.wait_ge(v_lo_ready, nth(n, b))
                pe.wait_ge(v_hi_ready, nth(n, b))
                if b:
                    pe.wait_ge(x1_ready, nth(n, b) - 1)
                else:
                    pe.wait_ge(ctxT_lo_ready, nth(n, b) + 1)
                product(ctx_bank[:], [(probs_hi[:, b, :], probs_lo[:, b, :], v_hi[:, b, :], v_lo[:, b, :])],
                        True, True).then_inc(attended, 1)

            def transpose_h(n, b):
                pe.wait_ge(h_ready, nth(n, b))
                if b:
                    pe.wait_ge(hT_lo_ready, nth(n, b) - 1)
                else:
                    pe.wait_ge(qT_lo_ready, nth(n, b) + 1)
                transposed(tok_bank, normed[:, b, :], hT_made)

            def transpose_fc1():
                pe.wait_ge(raw_loaded["fc1"], 16)
                for c in range(KL):
                    for k in range(KH):
                        mm = pe.transpose(up_bank[c][:, k * P:(k + 1) * P],
                                          raw[:, 0, k * LAT + c * P:k * LAT + (c + 1) * P], ident[:])
                    mm.then_inc(fc1T_made, 1)

            def fc1_expert():
                pe.wait_ge(fc1T_lo_ready, KL)
                pe.wait_ge(hi_ready["expert"], 1)
                pe.wait_ge(lo_ready["expert"], 1)
                for c in range(KL):
                    product(down_bank[c][:],
                            [(expert_hi[:, k, c * P:(c + 1) * P], expert_lo[:, k, c * P:(c + 1) * P],
                              lat_hi[:, k, :], lat_lo[:, k, :]) for k in range(KL)], True, True
                            ).then_inc(latW_made, 1)

            W_bank = [down_bank[0], down_bank[1], routed_bank, down_bank[0]]

            def make_W(c):
                if c == 0:
                    pe.wait_ge(latW_lo_ready, KL)
                    pe.wait_ge(hi_ready["fc2"], 1)
                    pe.wait_ge(lo_ready["fc2"], 1)
                if c == 3:
                    pe.wait_ge(W_lo_ready, 1)
                product(W_bank[c][:],
                        [(lat_hi[:, k, c * P:(c + 1) * P], lat_lo[:, k, c * P:(c + 1) * P],
                          fc2_hi[:, k, :], fc2_lo[:, k, :]) for k in range(KL)], True, True
                        ).then_inc(W_made, 1)

            def up(g, j):
                if j == 0:
                    pe.wait_ge(hT_lo_ready, nth(g, PAIR - 1))
                if not is_first(g) or j >= 2:
                    pe.wait_ge(relu_ready, UPS * g + j + 1 - 2)
                elif j == 0:
                    pe.wait_ge(fc1T_lo_ready, KL)
                pe.wait_ge(hi_ready[f"up{j}"], 1)
                pe.wait_ge(lo_ready[f"up{j}"], 1)
                for c in range(PAIR):
                    mm = product(up_bank[j % 2][:, c * GT:(c + 1) * GT],
                                 [(up_hi[:, j, k, c * P:(c + 1) * P], up_lo[:, j, k, c * P:(c + 1) * P],
                                   hT_hi[:, k, :], hT_lo[:, k, :]) for k in range(KH)], True, True)
                mm.then_inc(up_made, 1)

            def router(g, scores_read):
                pe.wait_ge(exp_ready, scores_read)
                pe.wait_ge(gate_lo_ready, 1)
                for b in range(PAIR):
                    to = small_bank[:, 2 * NE * b:2 * NE * (b + 1)]
                    for k in range(KH):
                        pe.matmul(to, hT_hi[:, k, tokens(b)], gate_hl[:, k, :, :].rearrange("p a e -> p (a e)"),
                                  start=(k == 0), stop=False)
                        mm = pe.matmul(to[:, 0:NE], hT_lo[:, k, tokens(b)], gate_hl[:, k, 0, :],
                                       start=False, stop=(k == KH - 1))
                mm.then_inc(logits_made, 1)

            def routed(g, b):
                if b == 0:
                    pe.wait_ge(W_lo_ready, KH)
                if b or not is_first(g):
                    pe.wait_ge(scaled_ready, nth(g, b) - 1)
                product(routed_bank[:],
                        [(hT_hi[:, k, tokens(b)], hT_lo[:, k, tokens(b)], W_hi[:, k, :], W_lo[:, k, :])
                         for k in range(KH)], True, True).then_inc(routed_made, 1)

            def down(g, b, half):
                if half == 0 and not is_first(g):
                    pe.wait_ge(y_ready, nth(g, b) - PAIR)
                for j in range(half * UPS // 2, (half + 1) * UPS // 2):
                    pe.wait_ge(act2_lo_ready, UPS * g + j + 1)
                    pe.wait_ge(hi_ready[f"down{j}"], 1)
                    pe.wait_ge(lo_ready[f"down{j}"], 1)
                    mm = product(down_bank[b][:],
                                 [(act2_hi[:, i, tokens(b)], act2_lo[:, i, tokens(b)],
                                   down_hi[:, i, :], down_lo[:, i, :]) for i in range(PAIR * j, PAIR * (j + 1))],
                                 j == 0, j == UPS - 1)
                if half == 1:
                    mm.then_inc(down_made, 1)

            def both(g):
                n = g + 1
                up(g, 0)
                transpose_ctx(n, 0)
                up(g, 1)
                transpose_q(n, 0)
                transpose_ctx(n, 1)
                up(g, 2)
                transpose_q(n, 1)
                scores(n, 0)
                up(g, 3)
                router(g, nth(n, 0))
                routed(g, 0)
                scores(n, 1)
                attend(n, 0)
                routed(g, 1)
                attend(n, 1)
                down(g, 0, 0)
                transpose_h(n, 0)
                down(g, 0, 1)
                down(g, 1, 0)
                transpose_h(n, 1)
                down(g, 1, 1)

            pe.wait_ge(ident_ready, 1)
            transpose_ctx(0, 0)
            transpose_q(0, 0)
            transpose_ctx(0, 1)
            transpose_q(0, 1)
            transpose_fc1()
            scores(0, 0)
            scores(0, 1)
            fc1_expert()
            attend(0, 0)
            make_W(0)
            attend(0, 1)
            make_W(1)
            transpose_h(0, 0)
            make_W(2)
            transpose_h(0, 1)
            make_W(3)
            both(0)
            with pe.Fori(1, GROUPS - 1) as g:
                both(g)
            g = GROUPS - 1
            for j in range(UPS):
                up(g, j)
            router(g, BATCH)
            for b in range(PAIR):
                routed(g, b)
            for b in range(PAIR):
                down(g, b, 0)
                down(g, b, 1)

        @block.scalar
        def _(act):
            def copied(to, src, ready):
                act.activation(to, src, ACT.Identity).then_inc(ready, 1)

            def split_hi(k):
                act.wait_ge(raw_loaded[k], 16)
                copied(piece[k][2], piece[k][1], hi_ready[k])

            def ctxT_hi_part(n, b):
                act.wait_ge(ctxT_made, nth(n, b))
                if not is_first(n):
                    act.wait_ge(scores_made, nth(n, b) - PAIR)
                copied(flat(ctxT_hi, b), ctx_bank[:], ctxT_hi_ready)

            def qT_hi_part(n, b):
                act.wait_ge(qT_made, nth(n, b))
                if not is_first(n):
                    act.wait_ge(scores_made, nth(n, b) - PAIR)
                copied(flat(qT_hi, b), tok_bank[:], qT_hi_ready)

            def exponentials(n, b):
                act.wait_ge(neg_max_ready, nth(n, b))
                if not is_first(n):
                    act.wait_ge(probs_lo_ready, nth(n, b) - PAIR)
                act.activation(probs[:, b, :], small_bank[:, 0:TOK], ACT.Exp, bias=neg_max[:, b, :], scale=SCALE,
                               accum_out=exp_sum[:, b, :]).then_inc(exp_ready, 1)

            def hT_hi_part(n, b):
                act.wait_ge(hT_made, nth(n, b))
                if not is_first(n):
                    act.wait_ge(routed_made, nth(n, b) - PAIR)
                copied(hT_hi[:, :, tokens(b)], tok_bank[:].rearrange("p (k t) -> p k t", k=KH), hT_hi_ready)

            def relu_squared(g, j):
                at = act2[:, j % 2, :, :].rearrange("p a t -> p (a t)")
                act.wait_ge(up_made, UPS * g + j + 1)
                if not is_first(g) or j >= 2:
                    act.wait_ge(act2_lo_ready, UPS * g + j + 1 - 2)
                act.activation(at, up_bank[j % 2][:], ACT.Relu).then_inc(relu_ready, 1)
                act.wait_ge(relu_ready, UPS * g + j + 1)
                act.activation(at, at, ACT.Square).then_inc(square_ready, 1)

            def scaled(g, b):
                act.wait_ge(routed_made, nth(g, b))
                act.wait_ge(route_ready, g + 1)
                if not is_first(g):
                    act.wait_ge(out_ready, nth(g, b) - PAIR)
                act.activation(y[:, b, :], routed_bank[:], ACT.Identity, scale=route[:, b:b + 1]
                               ).then_inc(scaled_ready, 1)

            def both(g, extra=()):
                n = g + 1
                relu_squared(g, 0)
                ctxT_hi_part(n, 0)
                split_some(extra, 0)
                relu_squared(g, 1)
                qT_hi_part(n, 0)
                ctxT_hi_part(n, 1)
                split_some(extra, 1)
                relu_squared(g, 2)
                qT_hi_part(n, 1)
                exponentials(n, 0)
                split_some(extra, 2)
                relu_squared(g, 3)
                split_some(extra, 3)
                scaled(g, 0)
                exponentials(n, 1)
                scaled(g, 1)
                hT_hi_part(n, 0)
                hT_hi_part(n, 1)

            def split_some(extra, at):
                if extra:
                    split_hi(extra[at])

            act.wait_ge(gates_loaded, 32)
            act.activation(gates[:], gates[:], ACT.Tanh).then_inc(tanh_ready, 1)
            ctxT_hi_part(0, 0)
            qT_hi_part(0, 0)
            ctxT_hi_part(0, 1)
            qT_hi_part(0, 1)
            split_hi("expert")
            for c in range(KL):
                act.wait_ge(fc1T_made, c + 1)
                copied(lat_hi[:, c, :], up_bank[c][:], fc1T_hi_ready)
            exponentials(0, 0)
            exponentials(0, 1)
            split_hi("fc2")
            split_hi("up0")
            for c in range(KL):
                act.wait_ge(latW_made, KL)
                copied(lat_hi[:, c, :], down_bank[c][:], latW_hi_ready)
            split_hi("up1")
            for c in range(2):
                act.wait_ge(W_made, c + 1)
                copied(W_hi[:, c, :], down_bank[c][:], W_hi_ready)
            hT_hi_part(0, 0)
            act.wait_ge(W_made, 3)
            copied(W_hi[:, 2, :], routed_bank[:], W_hi_ready)
            split_hi("up2")
            hT_hi_part(0, 1)
            act.wait_ge(W_made, 4)
            copied(W_hi[:, 3, :], down_bank[0][:], W_hi_ready)
            split_hi("up3")
            both(0, [f"down{j}" for j in range(UPS)])
            with act.Fori(1, GROUPS - 1) as g:
                both(g)
            g = GROUPS - 1
            for j in range(UPS):
                relu_squared(g, j)
            for b in range(PAIR):
                scaled(g, b)

        @block.vector
        def _(dve):
            def rest(to, whole, hi, ready):
                dve.tensor_tensor(to, whole, f32(hi), ALU.subtract).then_inc(ready, 1)

            def split_lo(k):
                dve.wait_ge(hi_ready[k], 1)
                rest(piece[k][3], piece[k][1], piece[k][2], lo_ready[k])

            def layernorm_stats(k, src, g, b):
                dve.bn_stats(stats[k][:, b, :], src).then_inc(stats_ready[k], 1)
                wait_apart(dve, stats_ready[k], nth(g, b))
                dve.bn_aggr(moments[k][:, b, :], stats[k][:, b, :]).then_inc(moments_ready[k], 1)
                dve.wait_ge(moments_ready[k], nth(g, b))
                dve.tensor_scalar(rstd[k][:, b, :], moments[k][:, b, 1:2], EPS, None, ALU.add
                                  ).then_inc(var_ready[k], 1)

            def q_stats(n, b):
                wait_apart(dve, x_loaded[b], 16 * (n + 1))
                layernorm_stats("x", xs[:, PAIR * n + b, :], n, b)

            def make_q(n, b):
                dve.wait_ge(rstd_ready["x"], nth(n, b))
                if not is_first(n):
                    dve.wait_ge(hT_made, nth(n, b) - PAIR)
                dve.tensor_scalar(normed[:, b, :], xs[:, PAIR * n + b, :], moments["x"][:, b, 0:1],
                                  rstd["x"][:, b, :], ALU.subtract, ALU.mult).then_inc(q_ready, 1)

            def v_hi_part(n, b):
                dve.wait_ge(ctx_loaded[b], 16 * (n + 1))
                if not is_first(n):
                    dve.wait_ge(attended, nth(n, b) - PAIR)
                dve.tensor_copy(v_hi[:, b, :], ctx[:, b, :]).then_inc(v_hi_ready, 1)

            def ctxT_lo_part(n, b):
                dve.wait_ge(ctxT_hi_ready, nth(n, b))
                rest(flat(ctxT_lo, b), ctx_bank[:], flat(ctxT_hi, b), ctxT_lo_ready)

            def qT_lo_part(n, b):
                dve.wait_ge(qT_hi_ready, nth(n, b))
                rest(flat(qT_lo, b), tok_bank[:], flat(qT_hi, b), qT_lo_ready)

            def score_max(n, b):
                dve.wait_ge(scores_made, nth(n, b))
                dve.tensor_reduce(row_max[:, b, :], small_bank[:, 0:TOK], AX.X, ALU.max).then_inc(row_max_ready, 1)
                dve.wait_ge(row_max_ready, nth(n, b))
                dve.tensor_scalar(neg_max[:, b, :], row_max[:, b, :], -SCALE, None, ALU.mult
                                  ).then_inc(neg_max_ready, 1)

            def make_probs(n, b):
                dve.wait_ge(exp_ready, nth(n, b))
                dve.reciprocal(exp_inv[:, b, :], exp_sum[:, b, :]).then_inc(exp_inv_ready, 1)
                dve.wait_ge(exp_inv_ready, nth(n, b))
                if is_first(n):
                    dve.wait_ge(tanh_ready, 1)
                dve.tensor_scalar(probs[:, b, :], probs[:, b, :], exp_inv[:, b, :], gates[:, 0:1],
                                  ALU.mult, ALU.mult).then_inc(probs_ready, 1)
                dve.wait_ge(probs_ready, nth(n, b))
                if not is_first(n):
                    dve.wait_ge(attended, nth(n, b) - PAIR)
                dve.tensor_copy(probs_hi[:, b, :], probs[:, b, :]).then_inc(probs_hi_ready, 1)
                dve.wait_ge(probs_hi_ready, nth(n, b))
                rest(probs_lo[:, b, :], probs[:, b, :], probs_hi[:, b, :], probs_lo_ready)

            def make_x1(n, b):
                at = xs[:, PAIR * n + b, :]
                dve.wait_ge(attended, nth(n, b))
                dve.tensor_tensor(at, at, ctx_bank[:], ALU.add).then_inc(x1_ready, 1)
                wait_apart(dve, x1_ready, nth(n, b))
                layernorm_stats("x1", at, n, b)

            def make_h(n, b):
                dve.wait_ge(rstd_ready["x1"], nth(n, b))
                dve.wait_ge(qT_made, nth(n, b))
                dve.tensor_scalar(normed[:, b, :], xs[:, PAIR * n + b, :], moments["x1"][:, b, 0:1],
                                  rstd["x1"][:, b, :], ALU.subtract, ALU.mult).then_inc(h_ready, 1)

            def hT_lo_part(n, b):
                dve.wait_ge(hT_hi_ready, nth(n, b))
                rest(hT_lo[:, :, tokens(b)], tok_bank[:].rearrange("p (k t) -> p k t", k=KH),
                     hT_hi[:, :, tokens(b)], hT_lo_ready)

            def square_parts(g, j):
                src = act2[:, j % 2, :, :].rearrange("p a t -> p (a t)")
                hi = flat(act2_hi, slice(PAIR * j, PAIR * (j + 1)))
                lo = flat(act2_lo, slice(PAIR * j, PAIR * (j + 1)))
                dve.wait_ge(square_ready, UPS * g + j + 1)
                if j == 0 and not is_first(g):
                    dve.wait_ge(down_made, PAIR * g)
                dve.tensor_copy(hi, src).then_inc(act2_hi_ready, 1)
                dve.wait_ge(act2_hi_ready, UPS * g + j + 1)
                rest(lo, src, hi, act2_lo_ready)

            def router_weight(g):
                dve.wait_ge(logits_made, g + 1)
                dve.tensor_reduce(logits[:].rearrange("p b e -> p (b e)").rearrange("p (b e) -> p b e", b=PAIR),
                                  small_bank[:, 0:PAIR * 2 * NE].rearrange("p (b a e) -> p b e a", b=PAIR, a=2),
                                  AX.X, ALU.add).then_inc(logits_ready, 1)
                for b in range(PAIR):
                    wait_apart(dve, logits_ready, g + 1)
                    dve.max(top8[:, b, :], logits[:, b, :]).then_inc(top_ready, 1)
                dve.wait_ge(top_ready, PAIR * g + PAIR)
                if not is_first(g):
                    dve.wait_ge(scaled_ready, PAIR * g)
                dve.tensor_reduce(route[:], top8[:, :, 0:2], AX.X, ALU.add).then_inc(route_ready, 1)

            def make_y(g, b):
                dve.wait_ge(down_made, nth(g, b))
                dve.wait_ge(scaled_ready, nth(g, b))
                dve.tensor_tensor(y[:, b, :], y[:, b, :], down_bank[b][:], ALU.add).then_inc(y_ready, 1)
                dve.wait_ge(y_ready, nth(g, b))
                layernorm_stats("y", y[:, b, :], g, b)

            def make_out(g, b):
                at = xs[:, PAIR * g + b, :]
                if is_first(g) and b == 0:
                    dve.wait_ge(affine_ready, 2)
                dve.scalar_tensor_tensor(out=y[:, b, :], in0=y[:, b, :], scalar=moments["y"][:, b, 0:1],
                                         in1=gamma[:], op0=ALU.subtract, op1=ALU.mult).then_inc(y_gamma_ready, 1)
                dve.wait_ge(y_gamma_ready, nth(g, b))
                dve.wait_ge(x1_beta_ready, nth(g, b))
                dve.wait_ge(rstd_ready["y"], nth(g, b))
                dve.scalar_tensor_tensor(out=at, in0=y[:, b, :], scalar=rstd["y"][:, b, :], in1=at,
                                         op0=ALU.mult, op1=ALU.add).then_inc(out_ready, 1)

            def both(g):
                n = g + 1
                q_stats(n, 0)
                v_hi_part(n, 0)
                make_q(n, 0)
                q_stats(n, 1)
                ctxT_lo_part(n, 0)
                square_parts(g, 0)
                make_q(n, 1)
                v_hi_part(n, 1)
                qT_lo_part(n, 0)
                ctxT_lo_part(n, 1)
                square_parts(g, 1)
                qT_lo_part(n, 1)
                score_max(n, 0)
                square_parts(g, 2)
                make_probs(n, 0)
                router_weight(g)
                square_parts(g, 3)
                score_max(n, 1)
                make_x1(n, 0)
                make_probs(n, 1)
                make_h(n, 0)
                make_x1(n, 1)
                hT_lo_part(n, 0)
                make_h(n, 1)
                make_y(g, 0)
                make_out(g, 0)
                hT_lo_part(n, 1)
                make_y(g, 1)
                make_out(g, 1)

            q_stats(0, 0)
            q_stats(0, 1)
            make_q(0, 0)
            make_q(0, 1)
            v_hi_part(0, 0)
            v_hi_part(0, 1)
            ctxT_lo_part(0, 0)
            qT_lo_part(0, 0)
            ctxT_lo_part(0, 1)
            qT_lo_part(0, 1)
            for c in range(KL):
                dve.wait_ge(fc1T_hi_ready, c + 1)
                rest(lat_lo[:, c, :], up_bank[c][:], lat_hi[:, c, :], fc1T_lo_ready)
            split_lo("expert")
            score_max(0, 0)
            score_max(0, 1)
            make_probs(0, 0)
            make_probs(0, 1)
            dve.wait_ge(gate_loaded, 16)
            dve.tensor_copy(gate_hl[:, :, 0, :], gate[:]).then_inc(gate_hi_ready, 1)
            dve.wait_ge(gate_hi_ready, 1)
            rest(gate_hl[:, :, 1, :], gate[:], gate_hl[:, :, 0, :], gate_lo_ready)
            make_x1(0, 0)
            for c in range(KL):
                dve.wait_ge(latW_hi_ready, c + 1)
                rest(lat_lo[:, c, :], down_bank[c][:], lat_hi[:, c, :], latW_lo_ready)
            make_x1(0, 1)
            make_h(0, 0)
            make_h(0, 1)
            split_lo("up0")
            for c in range(2):
                dve.wait_ge(W_hi_ready, c + 1)
                rest(W_lo[:, c, :], down_bank[c][:], W_hi[:, c, :], W_lo_ready)
            hT_lo_part(0, 0)
            dve.wait_ge(W_hi_ready, 3)
            rest(W_lo[:, 2, :], routed_bank[:], W_hi[:, 2, :], W_lo_ready)
            hT_lo_part(0, 1)
            dve.wait_ge(W_hi_ready, 4)
            rest(W_lo[:, 3, :], down_bank[0][:], W_hi[:, 3, :], W_lo_ready)
            split_lo("up2")
            both(0)
            with dve.Fori(1, GROUPS - 1) as g:
                both(g)
            g = GROUPS - 1
            for j in range(UPS):
                square_parts(g, j)
            router_weight(g)
            for b in range(PAIR):
                make_y(g, b)
                make_out(g, b)

        @block.gpsimd
        def _(pool):
            def split_lo(k):
                pool.wait_ge(hi_ready[k], 1)
                pool.tensor_tensor(piece[k][3], piece[k][1], f32(piece[k][2]), ALU.subtract
                                   ).then_inc(lo_ready[k], 1)

            def inverse_root(k, g, b):
                pool.wait_ge(var_ready[k], nth(g, b))
                pool.tensor_tensor(rstd[k][:, b, :], rstd[k][:, b, :], neg_half[:], ALU.pow
                                   ).then_inc(rstd_ready[k], 1)

            def v_lo_part(n, b):
                pool.wait_ge(v_hi_ready, nth(n, b))
                pool.tensor_tensor(v_lo[:, b, :], ctx[:, b, :], f32(v_hi[:, b, :]), ALU.subtract
                                   ).then_inc(v_lo_ready, 1)

            def add_beta(n, b):
                pool.wait_ge(h_ready, nth(n, b))
                if is_first(n) and b == 0:
                    pool.wait_ge(affine_ready, 2)
                at = xs[:, PAIR * n + b, :]
                pool.tensor_tensor(at, at, beta[:], ALU.add).then_inc(x1_beta_ready, 1)

            def both(g, extra=()):
                n = g + 1
                inverse_root("x", n, 0)
                v_lo_part(n, 0)
                inverse_root("x", n, 1)
                v_lo_part(n, 1)
                for k in extra:
                    split_lo(k)
                inverse_root("x1", n, 0)
                inverse_root("x1", n, 1)
                add_beta(n, 0)
                inverse_root("y", g, 0)
                add_beta(n, 1)
                inverse_root("y", g, 1)

            pool.memset(neg_half[:], -0.5).then_inc(half_ready, 1)
            pool.memset(ident[:], 0.0).then_inc(ident_zeroed, 1)
            pool.wait_ge(ident_zeroed, 1)
            pool.affine_select(out=ident[:], in_=ident[:], compare_op=ALU.not_equal, fill=1.0, base=0,
                               pattern=[[-1, P]], channel_multiplier=1).then_inc(ident_ready, 1)
            pool.wait_ge(half_ready, 1)
            inverse_root("x", 0, 0)
            inverse_root("x", 0, 1)
            v_lo_part(0, 0)
            v_lo_part(0, 1)
            split_lo("fc2")
            inverse_root("x1", 0, 0)
            inverse_root("x1", 0, 1)
            split_lo("up1")
            split_lo("up3")
            pool.wait_ge(affine_loaded, 32)
            pool.wait_ge(tanh_ready, 1)
            for t in (gamma, beta):
                pool.tensor_scalar(t[:], t[:], gates[:, 1:2], None, ALU.mult).then_inc(affine_ready, 1)
            add_beta(0, 0)
            add_beta(0, 1)
            both(0, [f"down{j}" for j in range(UPS)])
            with pool.Fori(1, GROUPS - 1) as g:
                both(g)
            g = GROUPS - 1
            for b in range(PAIR):
                inverse_root("y", g, b)


_INS = ["x", "ctx_4096", "g_xattn", "g_ffn", "L0_ffn_gate_w", "L0_ffn_up_w", "L0_ffn_down_w", "L0_ffn_fc1_w",
        "L0_ffn_fc2_w", "L0_ffn_expert_w", "L0_ffn_ln_gamma", "L0_ffn_ln_beta"]


def kernel(**inputs):
    import numpy as _np
    import concourse.bacc as _bacc
    from concourse import mybir as _mybir
    from concourse.bass_utils import run_bass_kernel_spmd as _run

    nc = _bacc.Bacc("TRN2", target_bir_lowering=False, num_devices=1)
    arrays, args = {}, []
    for name in _INS:
        a = _np.ascontiguousarray(inputs[name])
        arrays[f"in_{name}_dram"] = a
        args.append(nc.dram_tensor(f"in_{name}_dram", a.shape, _mybir.dt.from_np(a.dtype), kind="ExternalInput").ap())
    shape = inputs["x"].shape
    args.append(nc.dram_tensor("out_dram", shape, _mybir.dt.float32, kind="ExternalOutput").ap())
    flamingo_block(nc, *args)
    r = _run(nc, [arrays], core_ids=[0])
    return r.results[0]["out_dram"]
```

```python
from contextlib import ExitStack

import concourse.bass as bass
from concourse import mybir

F32 = mybir.dt.float32
F32R = mybir.dt.float32r
ALU = mybir.AluOpType
ACT = mybir.ActivationFunctionType
AX = mybir.AxisListType

P = 128
PAIR = 2
EPS = 1e-5
RING = 4
WARM_UP = 8


def flamingo_block(nc, x, ctx_in, g_xattn, g_ffn, gate_w, up_w, down_w, fc1_w, fc2_w, expert_w,
                   ln_gamma, ln_beta, out):
    BATCH, TOK, HID = x.shape
    INNER = up_w.shape[1]
    LAT = fc1_w.shape[1]
    NE = gate_w.shape[1]
    KH = HID // P
    KI = INNER // P
    KL = LAT // P
    GROUPS = BATCH // PAIR
    GT = PAIR * TOK
    UPS = KI // PAIR
    HALF = HID // 2
    SCALE = float(TOK) ** -0.5
    assert TOK == P and HID == 512 and GT * PAIR == 512 and NE == 8

    def nth(n, b):
        return PAIR * n + b + 1

    def is_first(g):
        return isinstance(g, int) and g == 0

    stack = ExitStack()
    with stack:
        def sb(name, shape, dt=F32):
            return stack.enter_context(nc.sbuf_tensor(name, shape, dt))

        def bank(name):
            return stack.enter_context(nc.psum_tensor(name, [P, 512], F32))

        def sem(name):
            return stack.enter_context(nc.semaphore(name))

        up_bank = [bank("up_bank0"), bank("up_bank1")]
        down_bank = [bank("down_bank0"), bank("down_bank1")]
        routed_banks = stack.enter_context(nc.psum_tensor("routed_banks", [P, 2, 512], F32))
        ctx_bank = bank("ctx_bank")
        tok_bank = bank("tok_bank")

        xs = sb("xs", [P, BATCH, HID])
        ctx = sb("ctx", [P, PAIR, HID])
        v_hi = sb("v_hi", [P, PAIR, HID], F32R)
        v_lo = sb("v_lo", [P, PAIR, HID], F32R)
        ctxT_hi = sb("ctxT_hi", [P, PAIR, KH, TOK], F32R)
        ctxT_lo = sb("ctxT_lo", [P, PAIR, KH, TOK], F32R)
        qT_hi = sb("qT_hi", [P, PAIR, KH, TOK], F32R)
        qT_lo = sb("qT_lo", [P, PAIR, KH, TOK], F32R)
        normed = sb("normed", [P, PAIR, HID])
        hT_hi = sb("hT_hi", [P, KH, GT], F32R)
        hT_lo = sb("hT_lo", [P, KH, GT], F32R)
        act2 = sb("act2", [P, 2, PAIR, GT])
        act2_hi = sb("act2_hi", [P, KI, GT], F32R)
        act2_lo = sb("act2_lo", [P, KI, GT], F32R)
        y = sb("y", [P, PAIR, HID])
        probs = sb("probs", [P, PAIR, TOK])
        probs_hi = sb("probs_hi", [P, PAIR, TOK], F32R)
        probs_lo = sb("probs_lo", [P, PAIR, TOK], F32R)

        raw = sb("raw", [P, RING, 1024])
        raw_expert = sb("raw_expert", [P, KL * LAT])
        up_hi = sb("up_hi", [P, UPS, KH, PAIR * P], F32R)
        up_lo = sb("up_lo", [P, UPS, KH, PAIR * P], F32R)
        down_hi = sb("down_hi", [P, KI, HID], F32R)
        down_lo = sb("down_lo", [P, KI, HID], F32R)
        W_hi = sb("W_hi", [P, KH, 2, HALF + NE], F32R)
        W_lo = sb("W_lo", [P, KH, 2, HALF + NE], F32R)
        lat_hi = sb("lat_hi", [P, KL, HID], F32R)
        lat_lo = sb("lat_lo", [P, KL, HID], F32R)
        expert_hi = sb("expert_hi", [P, KL, LAT], F32R)
        expert_lo = sb("expert_lo", [P, KL, LAT], F32R)
        fc2_hi = sb("fc2_hi", [P, KL, HID], F32R)
        fc2_lo = sb("fc2_lo", [P, KL, HID], F32R)
        gate = sb("gate", [P, KH, NE])
        gamma = sb("gamma", [P, HID])
        beta = sb("beta", [P, HID])
        gates = sb("gates", [P, 2])
        ident = sb("ident", [P, P])
        neg_half = sb("neg_half", [P, 1])

        LNS = ("x", "x1", "y")
        stats = {k: sb(f"stats_{k}", [P, PAIR, 6]) for k in LNS}
        moments = {k: sb(f"moments_{k}", [P, PAIR, 2]) for k in LNS}
        rstd = {k: sb(f"rstd_{k}", [P, PAIR, 1]) for k in LNS}
        neg_max = sb("neg_max", [P, PAIR, 1])
        exp_sum = sb("exp_sum", [P, PAIR, 1])
        exp_inv = sb("exp_inv", [P, PAIR, 1])
        row_max = sb("row_max", [P, PAIR, 1])
        top8 = sb("top8", [P, PAIR, 8])
        route = sb("route", [P, PAIR])

        x_loaded = [sem(f"x_loaded{b}") for b in range(PAIR)]
        ctx_loaded = [sem(f"ctx_loaded{b}") for b in range(PAIR)]
        gates_loaded = sem("gates_loaded")
        gate_loaded = sem("gate_loaded")
        affine_loaded = sem("affine_loaded")
        PIECES = ["fc1", "up0", "up1", "fc2", "up2", "up3"] + [f"down{j}" for j in range(UPS)]
        raw_loaded = {k: sem(f"{k}_loaded") for k in PIECES + ["expert"]}
        out_stored = sem("out_stored")
        waits_passed = sem("waits_passed")
        ident_zeroed = sem("ident_zeroed")
        ident_ready = sem("ident_ready")
        half_ready = sem("half_ready")
        tanh_ready = sem("tanh_ready")
        affine_ready = sem("affine_ready")
        hi_ready = {k: sem(f"{k}_hi_ready") for k in PIECES[1:] + ["expert"]}
        lo_ready = {k: sem(f"{k}_lo_ready") for k in PIECES[1:] + ["expert"]}
        gate_hi_ready = sem("gate_hi_ready")
        gate_lo_ready = sem("gate_lo_ready")
        fc1T_made = sem("fc1T_made")
        fc1T_copied = sem("fc1T_copied")
        fc1T_hi_ready = sem("fc1T_hi_ready")
        fc1T_lo_ready = sem("fc1T_lo_ready")
        latW_made = sem("latW_made")
        latW_hi_ready = sem("latW_hi_ready")
        latW_lo_ready = sem("latW_lo_ready")
        W_made = sem("W_made")
        W_hi_ready = sem("W_hi_ready")
        W_lo_ready = sem("W_lo_ready")
        stats_ready = {k: sem(f"stats_{k}_ready") for k in LNS}
        moments_ready = {k: sem(f"moments_{k}_ready") for k in LNS}
        var_ready = {k: sem(f"var_{k}_ready") for k in LNS}
        rstd_ready = {k: sem(f"rstd_{k}_ready") for k in LNS}
        q_ready = sem("q_ready")
        v_hi_ready = sem("v_hi_ready")
        v_lo_ready = sem("v_lo_ready")
        ctxT_made = sem("ctxT_made")
        ctxT_hi_ready = sem("ctxT_hi_ready")
        ctxT_lo_ready = sem("ctxT_lo_ready")
        qT_made = sem("qT_made")
        qT_hi_ready = sem("qT_hi_ready")
        qT_lo_ready = sem("qT_lo_ready")
        scores_made = sem("scores_made")
        row_max_ready = sem("row_max_ready")
        neg_max_ready = sem("neg_max_ready")
        exp_ready = sem("exp_ready")
        exp_inv_ready = sem("exp_inv_ready")
        probs_ready = sem("probs_ready")
        probs_hi_ready = sem("probs_hi_ready")
        probs_lo_ready = sem("probs_lo_ready")
        attended = sem("attended")
        x1_ready = sem("x1_ready")
        h_ready = sem("h_ready")
        hT_made = sem("hT_made")
        hT_hi_ready = sem("hT_hi_ready")
        hT_lo_ready = sem("hT_lo_ready")
        up_made = sem("up_made")
        relu_ready = sem("relu_ready")
        square_ready = sem("square_ready")
        act2_hi_ready = sem("act2_hi_ready")
        act2_lo_ready = sem("act2_lo_ready")
        top_ready = sem("top_ready")
        route_ready = sem("route_ready")
        routed_made = sem("routed_made")
        scaled_ready = sem("scaled_ready")
        down_made = sem("down_made")
        y_ready = sem("y_ready")
        x1_beta_ready = sem("x1_beta_ready")
        y_gamma_ready = sem("y_gamma_ready")
        out_ready = sem("out_ready")

        def flat(t, *at):
            v = t[(slice(None),) + at]
            return v.rearrange("p a b -> p (a b)") if len(v.shape) == 3 else v

        def slot(k, size):
            return raw[:, PIECES.index(k) % RING, 0:size]

        piece = {
            "fc1": (fc1_w.rearrange("(k p) l -> p k l", p=P), slot("fc1", KH * LAT), None, None),
            "expert": (expert_w.rearrange("(k p) l -> p k l", p=P), raw_expert[:],
                       flat(expert_hi), flat(expert_lo)),
            "fc2": (fc2_w.rearrange("(k p) n -> p k n", p=P), slot("fc2", KL * HID), flat(fc2_hi), flat(fc2_lo)),
        }
        for j in range(UPS):
            piece[f"up{j}"] = (up_w.rearrange("(k p) i -> p k i", p=P)[:, :, j * PAIR * P:(j + 1) * PAIR * P],
                               slot(f"up{j}", KH * PAIR * P), flat(up_hi, j), flat(up_lo, j))
            piece[f"down{j}"] = (down_w.rearrange("(k p) n -> p k n", p=P)[:, PAIR * j:PAIR * (j + 1), :],
                                 slot(f"down{j}", PAIR * HID), flat(down_hi, slice(PAIR * j, PAIR * (j + 1))),
                                 flat(down_lo, slice(PAIR * j, PAIR * (j + 1))))

        def f32(ap):
            return ap.bitcast(F32)

        def turned_ctx_bank(n, b):
            return up_bank[0] if is_first(n) and b else ctx_bank

        def turned_q_bank(n, b):
            return up_bank[1] if is_first(n) and b else tok_bank

        W_bank = [routed_banks[:, 0, :], routed_banks[:, 1, :], down_bank[0][:], down_bank[1][:]]

        def W_halves(t, c):
            return t[:, c, :, 0:HALF]

        def halves(ap):
            return ap.rearrange("p (a n) -> p a n", a=2)

        def tokens(b):
            return slice(b * TOK, (b + 1) * TOK)

        def wait_apart(engine, on, value):
            engine.wait_ge(on, value)
            engine.sem_inc(waits_passed, 1)

        block = stack.enter_context(nc.Block())

        @block.sync
        def _(sp):
            def load_x(n, b):
                if not is_first(n):
                    sp.wait_ge(stats_ready["x"], nth(n, b) - PAIR)
                sp.dma_start(xs[:, PAIR * n + b, :], x[PAIR * n + b]).then_inc(x_loaded[b], 16)

            def load_ctx(n, b):
                if not is_first(n):
                    sp.wait_ge(v_hi_ready, nth(n, b) - PAIR)
                    sp.wait_ge(v_lo_ready, nth(n, b) - PAIR)
                    sp.wait_ge(ctxT_made, nth(n, b) - PAIR)
                sp.dma_start(ctx[:, b, :], ctx_in[PAIR * n + b]).then_inc(ctx_loaded[b], 16)

            def load_piece(k):
                at = 0 if k == "expert" else PIECES.index(k)
                if at >= RING:
                    before = PIECES[at - RING]
                    if before == "fc1":
                        sp.wait_ge(fc1T_made, KL)
                    else:
                        sp.wait_ge(hi_ready[before], 1)
                        sp.wait_ge(lo_ready[before], 1)
                src, dst, _, _ = piece[k]
                sp.dma_start(dst.rearrange("p (k n) -> p k n", k=src.shape[1]), src).then_inc(raw_loaded[k], 16)

            def store(g, b):
                sp.wait_ge(out_ready, nth(g, b))
                sp.dma_start(out[PAIR * g + b], xs[:, PAIR * g + b, :]).then_inc(out_stored, 16)

            load_x(0, 0)
            load_ctx(0, 0)
            load_x(0, 1)
            load_ctx(0, 1)
            load_piece("fc1")
            for g_at, g_in in enumerate((g_xattn, g_ffn)):
                sp.dma_start(gates[:, g_at:g_at + 1], g_in.rearrange("(a d) -> a d", a=1).to_broadcast([P, 1])
                             ).then_inc(gates_loaded, 16)
            load_piece("expert")
            load_piece("up0")
            load_piece("up1")
            load_piece("fc2")
            sp.dma_start(gate[:], gate_w.rearrange("(k p) e -> p k e", p=P)).then_inc(gate_loaded, 16)
            load_piece("up2")
            for b in range(PAIR):
                load_x(1, b)
                load_ctx(1, b)
            for t, src in ((gamma, ln_gamma), (beta, ln_beta)):
                sp.dma_start(t[:], src.rearrange("(a d) -> a d", a=1).to_broadcast([P, HID])
                             ).then_inc(affine_loaded, 16)
            for k in PIECES[5:]:
                load_piece(k)
            with sp.Fori(0, GROUPS - 2) as g:
                for b in range(PAIR):
                    sp.wait_ge(stats_ready["x"], PAIR * g + b + 1 + PAIR)
                    sp.dma_start(xs[:, PAIR * g + 2 * PAIR + b, :], x[PAIR * g + 2 * PAIR + b]
                                 ).then_inc(x_loaded[b], 16)
                    load_ctx(g + 2, b)
                for b in range(PAIR):
                    store(g, b)
            for g in range(GROUPS - 2, GROUPS):
                for b in range(PAIR):
                    store(g, b)
            sp.wait_ge(out_stored, 16 * BATCH)

        @block.tensor
        def _(pe):
            def product(to, parts, first, last):
                mm = None
                for at, (a_hi, a_lo, b_hi, b_lo) in enumerate(parts):
                    begins, ends = first and at == 0, last and at == len(parts) - 1
                    pe.matmul(to, a_hi, b_hi, start=begins, stop=False)
                    pe.matmul(to, a_hi, b_lo, start=False, stop=False)
                    mm = pe.matmul(to, a_lo, b_hi, start=False, stop=ends)
                return mm

            def transposed(to, src, made):
                for k in range(KH):
                    mm = pe.transpose(to[:, k * P:(k + 1) * P], src[:, k * P:(k + 1) * P], ident[:])
                mm.then_inc(made, 1)

            def transpose_ctx(n, b):
                pe.wait_ge(ctx_loaded[b], 16 * (n + 1))
                if not is_first(n):
                    pe.wait_ge(ctxT_lo_ready if b else x1_ready, nth(n, b) - 1)
                transposed(turned_ctx_bank(n, b), ctx[:, b, :], ctxT_made)

            def transpose_q(n, b):
                pe.wait_ge(q_ready, nth(n, b))
                if not is_first(n):
                    pe.wait_ge(qT_lo_ready if b else hT_lo_ready, nth(n, b) - 1)
                transposed(turned_q_bank(n, b), normed[:, b, :], qT_made)

            def scores(n, b):
                pe.wait_ge(qT_lo_ready, nth(n, b))
                pe.wait_ge(ctxT_lo_ready, nth(n, b))
                if not isinstance(n, int) or n > 1:
                    pe.wait_ge(y_ready, nth(n, b) - 2 * PAIR)
                elif n == 1:
                    pe.wait_ge(W_lo_ready, 3 + b)
                product(down_bank[b][:, 0:TOK],
                        [(qT_hi[:, b, k, :], qT_lo[:, b, k, :], ctxT_hi[:, b, k, :], ctxT_lo[:, b, k, :])
                         for k in range(KH)], True, True).then_inc(scores_made, 1)

            def attend(n, b):
                pe.wait_ge(probs_lo_ready, nth(n, b))
                pe.wait_ge(v_lo_ready, nth(n, b))
                pe.wait_ge(v_hi_ready, nth(n, b))
                if b:
                    pe.wait_ge(x1_ready, nth(n, b) - 1)
                else:
                    pe.wait_ge(ctxT_lo_ready, nth(n, b) + 1)
                product(ctx_bank[:], [(probs_hi[:, b, :], probs_lo[:, b, :], v_hi[:, b, :], v_lo[:, b, :])],
                        True, True).then_inc(attended, 1)

            def transpose_h(n, b):
                pe.wait_ge(h_ready, nth(n, b))
                if b:
                    pe.wait_ge(hT_lo_ready, nth(n, b) - 1)
                else:
                    pe.wait_ge(qT_lo_ready, nth(n, b) + 1)
                transposed(tok_bank, normed[:, b, :], hT_made)

            def transpose_fc1(c):
                pe.wait_ge(raw_loaded["fc1"], 16)
                pe.wait_ge(qT_lo_ready if c else ctxT_lo_ready, 2)
                for k in range(KH):
                    mm = pe.transpose(up_bank[c][:, k * P:(k + 1) * P],
                                      raw[:, 0, k * LAT + c * P:k * LAT + (c + 1) * P], ident[:])
                mm.then_inc(fc1T_made, 1)

            def fc1_expert(c):
                pe.wait_ge(fc1T_lo_ready, KL)
                pe.wait_ge(hi_ready["expert"], 1)
                pe.wait_ge(lo_ready["expert"], 1)
                product(routed_banks[:, c, :],
                        [(expert_hi[:, k, c * P:(c + 1) * P], expert_lo[:, k, c * P:(c + 1) * P],
                          lat_hi[:, k, :], lat_lo[:, k, :]) for k in range(KL)], True, True
                        ).then_inc(latW_made, 1)

            def make_W(c):
                pe.wait_ge(latW_lo_ready, KL)
                pe.wait_ge(hi_ready["fc2"], 1)
                pe.wait_ge(lo_ready["fc2"], 1)
                if c >= 2:
                    pe.wait_ge(exp_ready, c - 1)
                product(W_bank[c],
                        [(lat_hi[:, k, c * P:(c + 1) * P], lat_lo[:, k, c * P:(c + 1) * P],
                          fc2_hi[:, k, :], fc2_lo[:, k, :]) for k in range(KL)], True, True
                        ).then_inc(W_made, 1)

            def up(g, j):
                if j == 0:
                    pe.wait_ge(hT_lo_ready, nth(g, PAIR - 1))
                if not is_first(g) or j >= 2:
                    pe.wait_ge(relu_ready, UPS * g + j + 1 - 2)
                elif j == 0:
                    pe.wait_ge(fc1T_copied, KL)
                pe.wait_ge(hi_ready[f"up{j}"], 1)
                pe.wait_ge(lo_ready[f"up{j}"], 1)
                for c in range(PAIR):
                    mm = product(up_bank[j % 2][:, c * GT:(c + 1) * GT],
                                 [(up_hi[:, j, k, c * P:(c + 1) * P], up_lo[:, j, k, c * P:(c + 1) * P],
                                   hT_hi[:, k, :], hT_lo[:, k, :]) for k in range(KH)], True, True)
                mm.then_inc(up_made, 1)

            def routed(g, b):
                if b == 0:
                    pe.wait_ge(W_lo_ready, KH)
                    pe.wait_ge(gate_lo_ready, 1)
                if b or not is_first(g):
                    pe.wait_ge(scaled_ready, nth(g, b) - 1)
                for a, size in enumerate((HALF + NE, HALF)):
                    mm = product(routed_banks[:, a, 0:size],
                                 [(hT_hi[:, k, tokens(b)], hT_lo[:, k, tokens(b)],
                                   W_hi[:, k, a, 0:size], W_lo[:, k, a, 0:size]) for k in range(KH)], True, True)
                mm.then_inc(routed_made, 1)

            def down(g, b, half, scores_read=None):
                if half == 0:
                    pe.wait_ge(exp_ready, scores_read)
                for j in range(half * UPS // 2, (half + 1) * UPS // 2):
                    pe.wait_ge(act2_lo_ready, UPS * g + j + 1)
                    pe.wait_ge(hi_ready[f"down{j}"], 1)
                    pe.wait_ge(lo_ready[f"down{j}"], 1)
                    mm = product(down_bank[b][:],
                                 [(act2_hi[:, i, tokens(b)], act2_lo[:, i, tokens(b)],
                                   down_hi[:, i, :], down_lo[:, i, :]) for i in range(PAIR * j, PAIR * (j + 1))],
                                 j == 0, j == UPS - 1)
                if half == 1:
                    mm.then_inc(down_made, 1)

            def both(g):
                n = g + 1
                up(g, 0)
                transpose_ctx(n, 0)
                if is_first(g):
                    fc1_expert(1)
                up(g, 1)
                transpose_ctx(n, 1)
                up(g, 2)
                up(g, 3)
                transpose_q(n, 0)
                if is_first(g):
                    for c in range(KH):
                        make_W(c)
                routed(g, 0)
                transpose_q(n, 1)
                scores(n, 0)
                routed(g, 1)
                scores(n, 1)
                attend(n, 0)
                down(g, 0, 0, nth(n, 0))
                attend(n, 1)
                down(g, 0, 1)
                transpose_h(n, 0)
                down(g, 1, 0, nth(n, 1))
                transpose_h(n, 1)
                down(g, 1, 1)

            pe.wait_ge(ident_ready, 1)
            for _ in range(WARM_UP):
                pe.matmul(up_bank[0][:, 0:P], ident[:], ident[:], start=True, stop=True)
            transpose_ctx(0, 0)
            transpose_q(0, 0)
            transpose_ctx(0, 1)
            transpose_q(0, 1)
            scores(0, 0)
            transpose_fc1(0)
            scores(0, 1)
            transpose_fc1(1)
            attend(0, 0)
            attend(0, 1)
            fc1_expert(0)
            transpose_h(0, 0)
            transpose_h(0, 1)
            both(0)
            with pe.Fori(1, GROUPS - 1) as g:
                both(g)
            g = GROUPS - 1
            for j in range(UPS):
                up(g, j)
            for b in range(PAIR):
                routed(g, b)
                pe.wait_ge(y_ready, nth(g, b) - PAIR)
                down(g, b, 0, BATCH)
                down(g, b, 1)

        @block.scalar
        def _(act):
            def copied(to, src, ready):
                act.activation(to, src, ACT.Identity).then_inc(ready, 1)

            def split_hi(k):
                act.wait_ge(raw_loaded[k], 16)
                copied(piece[k][2], piece[k][1], hi_ready[k])

            def ctxT_hi_part(n, b):
                act.wait_ge(ctxT_made, nth(n, b))
                if not is_first(n):
                    act.wait_ge(scores_made, nth(n, b) - PAIR)
                copied(flat(ctxT_hi, b), turned_ctx_bank(n, b)[:], ctxT_hi_ready)

            def qT_hi_part(n, b):
                act.wait_ge(qT_made, nth(n, b))
                if not is_first(n):
                    act.wait_ge(scores_made, nth(n, b) - PAIR)
                copied(flat(qT_hi, b), turned_q_bank(n, b)[:], qT_hi_ready)

            def v_hi_part(n, b):
                act.wait_ge(ctx_loaded[b], 16 * (n + 1))
                if not is_first(n):
                    act.wait_ge(attended, nth(n, b) - PAIR)
                copied(v_hi[:, b, :], ctx[:, b, :], v_hi_ready)

            def exponentials(n, b):
                act.wait_ge(neg_max_ready, nth(n, b))
                if not is_first(n):
                    act.wait_ge(probs_lo_ready, nth(n, b) - PAIR)
                act.activation(probs[:, b, :], down_bank[b][:, 0:TOK], ACT.Exp, bias=neg_max[:, b, :], scale=SCALE,
                               accum_out=exp_sum[:, b, :]).then_inc(exp_ready, 1)

            def hT_hi_part(n, b):
                act.wait_ge(hT_made, nth(n, b))
                if not is_first(n):
                    act.wait_ge(routed_made, nth(n, b) - PAIR)
                copied(hT_hi[:, :, tokens(b)], tok_bank[:].rearrange("p (k t) -> p k t", k=KH), hT_hi_ready)

            def relu_squared(g, j):
                at = act2[:, j % 2, :, :].rearrange("p a t -> p (a t)")
                act.wait_ge(up_made, UPS * g + j + 1)
                if not is_first(g) or j >= 2:
                    act.wait_ge(act2_lo_ready, UPS * g + j + 1 - 2)
                act.activation(at, up_bank[j % 2][:], ACT.Relu).then_inc(relu_ready, 1)
                act.wait_ge(relu_ready, UPS * g + j + 1)
                if j == 0 and not is_first(g):
                    act.wait_ge(down_made, PAIR * g)
                act.activation(flat(act2_hi, slice(PAIR * j, PAIR * (j + 1))), at, ACT.Square
                               ).then_inc(act2_hi_ready, 1)
                act.wait_ge(act2_hi_ready, UPS * g + j + 1)
                act.activation(at, at, ACT.Square).then_inc(square_ready, 1)

            def scaled(g, b):
                act.wait_ge(routed_made, nth(g, b))
                act.wait_ge(route_ready, nth(g, b))
                if not is_first(g):
                    act.wait_ge(out_ready, nth(g, b) - PAIR)
                act.activation(halves(y[:, b, :]), routed_banks[:, :, 0:HALF], ACT.Identity, scale=route[:, b:b + 1]
                               ).then_inc(scaled_ready, 1)

            def latW_hi_part():
                for c in range(KL):
                    act.wait_ge(latW_made, KL)
                    copied(lat_hi[:, c, :], routed_banks[:, c, :], latW_hi_ready)

            def both(g):
                n = g + 1
                relu_squared(g, 0)
                ctxT_hi_part(n, 0)
                v_hi_part(n, 0)
                if is_first(g):
                    latW_hi_part()
                    split_hi("up3")
                relu_squared(g, 1)
                ctxT_hi_part(n, 1)
                v_hi_part(n, 1)
                relu_squared(g, 2)
                if is_first(g):
                    split_hi("down0")
                relu_squared(g, 3)
                qT_hi_part(n, 0)
                if is_first(g):
                    for c in range(KH):
                        act.wait_ge(W_made, c + 1)
                        copied(W_halves(W_hi, c), halves(W_bank[c]), W_hi_ready)
                    split_hi("down1")
                    split_hi("down2")
                scaled(g, 0)
                qT_hi_part(n, 1)
                if is_first(g):
                    split_hi("down3")
                exponentials(n, 0)
                scaled(g, 1)
                exponentials(n, 1)
                hT_hi_part(n, 0)
                hT_hi_part(n, 1)

            ctxT_hi_part(0, 0)
            v_hi_part(0, 0)
            qT_hi_part(0, 0)
            ctxT_hi_part(0, 1)
            v_hi_part(0, 1)
            qT_hi_part(0, 1)
            act.wait_ge(gates_loaded, 32)
            act.activation(gates[:], gates[:], ACT.Tanh).then_inc(tanh_ready, 1)
            split_hi("expert")
            split_hi("up0")
            for c in range(KL):
                exponentials(0, c)
                act.wait_ge(fc1T_made, c + 1)
                copied(lat_hi[:, c, :], up_bank[c][:], fc1T_hi_ready)
                copied(y[:, c, :], up_bank[c][:], fc1T_copied)
            split_hi("up1")
            split_hi("fc2")
            split_hi("up2")
            hT_hi_part(0, 0)
            hT_hi_part(0, 1)
            act.wait_ge(affine_loaded, 32)
            act.wait_ge(tanh_ready, 1)
            for t in (gamma, beta):
                act.activation(t[:], t[:], ACT.Identity, scale=gates[:, 1:2]).then_inc(affine_ready, 1)
            both(0)
            with act.Fori(1, GROUPS - 1) as g:
                both(g)
            g = GROUPS - 1
            for j in range(UPS):
                relu_squared(g, j)
            for b in range(PAIR):
                scaled(g, b)

        @block.vector
        def _(dve):
            def rest(to, whole, hi, ready):
                dve.tensor_tensor(to, whole, f32(hi), ALU.subtract).then_inc(ready, 1)

            def split_lo(k):
                dve.wait_ge(hi_ready[k], 1)
                rest(piece[k][3], piece[k][1], piece[k][2], lo_ready[k])

            def layernorm_stats(k, src, g, b):
                dve.bn_stats(stats[k][:, b, :], src).then_inc(stats_ready[k], 1)
                wait_apart(dve, stats_ready[k], nth(g, b))
                dve.bn_aggr(moments[k][:, b, :], stats[k][:, b, :]).then_inc(moments_ready[k], 1)
                dve.wait_ge(moments_ready[k], nth(g, b))
                dve.tensor_scalar(rstd[k][:, b, :], moments[k][:, b, 1:2], EPS, None, ALU.add
                                  ).then_inc(var_ready[k], 1)

            def q_stats(n, b):
                wait_apart(dve, x_loaded[b], 16 * (n + 1))
                layernorm_stats("x", xs[:, PAIR * n + b, :], n, b)

            def make_q(n, b):
                dve.wait_ge(rstd_ready["x"], nth(n, b))
                if not is_first(n):
                    dve.wait_ge(hT_made, nth(n, b) - PAIR)
                dve.tensor_scalar(normed[:, b, :], xs[:, PAIR * n + b, :], moments["x"][:, b, 0:1],
                                  rstd["x"][:, b, :], ALU.subtract, ALU.mult).then_inc(q_ready, 1)

            def ctxT_lo_part(n, b):
                dve.wait_ge(ctxT_hi_ready, nth(n, b))
                rest(flat(ctxT_lo, b), turned_ctx_bank(n, b)[:], flat(ctxT_hi, b), ctxT_lo_ready)

            def qT_lo_part(n, b):
                dve.wait_ge(qT_hi_ready, nth(n, b))
                rest(flat(qT_lo, b), turned_q_bank(n, b)[:], flat(qT_hi, b), qT_lo_ready)

            def score_max(n, b):
                dve.wait_ge(scores_made, nth(n, b))
                dve.tensor_reduce(row_max[:, b, :], down_bank[b][:, 0:TOK], AX.X, ALU.max).then_inc(row_max_ready, 1)
                dve.wait_ge(row_max_ready, nth(n, b))
                dve.tensor_scalar(neg_max[:, b, :], row_max[:, b, :], -SCALE, None, ALU.mult
                                  ).then_inc(neg_max_ready, 1)

            def make_probs(n, b):
                dve.wait_ge(exp_ready, nth(n, b))
                dve.reciprocal(exp_inv[:, b, :], exp_sum[:, b, :]).then_inc(exp_inv_ready, 1)
                dve.wait_ge(exp_inv_ready, nth(n, b))
                if is_first(n):
                    dve.wait_ge(tanh_ready, 1)
                dve.tensor_scalar(probs[:, b, :], probs[:, b, :], exp_inv[:, b, :], gates[:, 0:1],
                                  ALU.mult, ALU.mult).then_inc(probs_ready, 1)
                dve.wait_ge(probs_ready, nth(n, b))
                if not is_first(n):
                    dve.wait_ge(attended, nth(n, b) - PAIR)
                dve.tensor_copy(probs_hi[:, b, :], probs[:, b, :]).then_inc(probs_hi_ready, 1)
                dve.wait_ge(probs_hi_ready, nth(n, b))
                rest(probs_lo[:, b, :], probs[:, b, :], probs_hi[:, b, :], probs_lo_ready)

            def make_x1(n, b):
                at = xs[:, PAIR * n + b, :]
                dve.wait_ge(attended, nth(n, b))
                dve.tensor_tensor(at, at, ctx_bank[:], ALU.add).then_inc(x1_ready, 1)
                wait_apart(dve, x1_ready, nth(n, b))
                layernorm_stats("x1", at, n, b)

            def make_h(n, b):
                dve.wait_ge(rstd_ready["x1"], nth(n, b))
                dve.wait_ge(qT_made, nth(n, b))
                dve.tensor_scalar(normed[:, b, :], xs[:, PAIR * n + b, :], moments["x1"][:, b, 0:1],
                                  rstd["x1"][:, b, :], ALU.subtract, ALU.mult).then_inc(h_ready, 1)

            def hT_lo_part(n, b):
                dve.wait_ge(hT_hi_ready, nth(n, b))
                rest(hT_lo[:, :, tokens(b)], tok_bank[:].rearrange("p (k t) -> p k t", k=KH),
                     hT_hi[:, :, tokens(b)], hT_lo_ready)

            def square_lo_part(g, j):
                src = act2[:, j % 2, :, :].rearrange("p a t -> p (a t)")
                hi = flat(act2_hi, slice(PAIR * j, PAIR * (j + 1)))
                lo = flat(act2_lo, slice(PAIR * j, PAIR * (j + 1)))
                dve.wait_ge(square_ready, UPS * g + j + 1)
                if j == 0 and not is_first(g):
                    dve.wait_ge(down_made, PAIR * g)
                rest(lo, src, hi, act2_lo_ready)

            def router_weight(g, b):
                wait_apart(dve, routed_made, nth(g, b))
                dve.max(top8[:, b, :], routed_banks[:, 0, HALF:HALF + NE]).then_inc(top_ready, 1)
                dve.wait_ge(top_ready, nth(g, b))
                if not is_first(g):
                    dve.wait_ge(scaled_ready, nth(g, b) - PAIR)
                dve.tensor_reduce(route[:, b:b + 1], top8[:, b, 0:2], AX.X, ALU.add).then_inc(route_ready, 1)

            def make_y(g, b):
                dve.wait_ge(down_made, nth(g, b))
                dve.wait_ge(scaled_ready, nth(g, b))
                dve.tensor_tensor(y[:, b, :], y[:, b, :], down_bank[b][:], ALU.add).then_inc(y_ready, 1)
                dve.wait_ge(y_ready, nth(g, b))
                layernorm_stats("y", y[:, b, :], g, b)

            def make_out(g, b):
                at = xs[:, PAIR * g + b, :]
                if is_first(g) and b == 0:
                    dve.wait_ge(affine_ready, 2)
                dve.scalar_tensor_tensor(out=y[:, b, :], in0=y[:, b, :], scalar=moments["y"][:, b, 0:1],
                                         in1=gamma[:], op0=ALU.subtract, op1=ALU.mult).then_inc(y_gamma_ready, 1)
                dve.wait_ge(y_gamma_ready, nth(g, b))
                dve.wait_ge(x1_beta_ready, nth(g, b))
                dve.wait_ge(rstd_ready["y"], nth(g, b))
                dve.scalar_tensor_tensor(out=at, in0=y[:, b, :], scalar=rstd["y"][:, b, :], in1=at,
                                         op0=ALU.mult, op1=ALU.add).then_inc(out_ready, 1)

            def both(g):
                n = g + 1
                q_stats(n, 0)
                ctxT_lo_part(n, 0)
                square_lo_part(g, 0)
                if is_first(g):
                    for c in range(KL):
                        dve.wait_ge(latW_hi_ready, c + 1)
                        rest(lat_lo[:, c, :], routed_banks[:, c, :], lat_hi[:, c, :], latW_lo_ready)
                make_q(n, 0)
                q_stats(n, 1)
                if is_first(g):
                    split_lo("up3")
                ctxT_lo_part(n, 1)
                square_lo_part(g, 1)
                make_q(n, 1)
                square_lo_part(g, 2)
                square_lo_part(g, 3)
                qT_lo_part(n, 0)
                if is_first(g):
                    for c in range(KH):
                        dve.wait_ge(W_hi_ready, c + 1)
                        rest(W_halves(W_lo, c), halves(W_bank[c]), W_halves(W_hi, c), W_lo_ready)
                    split_lo("down1")
                router_weight(g, 0)
                qT_lo_part(n, 1)
                if is_first(g):
                    split_lo("down3")
                score_max(n, 0)
                make_probs(n, 0)
                router_weight(g, 1)
                score_max(n, 1)
                make_probs(n, 1)
                make_x1(n, 0)
                make_h(n, 0)
                make_x1(n, 1)
                make_h(n, 1)
                hT_lo_part(n, 0)
                make_y(g, 0)
                hT_lo_part(n, 1)
                make_out(g, 0)
                make_y(g, 1)
                make_out(g, 1)

            q_stats(0, 0)
            make_q(0, 0)
            q_stats(0, 1)
            ctxT_lo_part(0, 0)
            make_q(0, 1)
            qT_lo_part(0, 0)
            ctxT_lo_part(0, 1)
            qT_lo_part(0, 1)
            score_max(0, 0)
            make_probs(0, 0)
            score_max(0, 1)
            make_probs(0, 1)
            make_x1(0, 0)
            make_h(0, 0)
            make_x1(0, 1)
            hT_lo_part(0, 0)
            make_h(0, 1)
            dve.wait_ge(gate_loaded, 16)
            dve.tensor_copy(W_hi[:, :, 0, HALF:HALF + NE], gate[:]).then_inc(gate_hi_ready, 1)
            dve.wait_ge(gate_hi_ready, 1)
            rest(W_lo[:, :, 0, HALF:HALF + NE], gate[:], W_hi[:, :, 0, HALF:HALF + NE], gate_lo_ready)
            hT_lo_part(0, 1)
            both(0)
            with dve.Fori(1, GROUPS - 1) as g:
                both(g)
            g = GROUPS - 1
            for j in range(UPS):
                square_lo_part(g, j)
            for b in range(PAIR):
                router_weight(g, b)
            for b in range(PAIR):
                make_y(g, b)
                make_out(g, b)

        @block.gpsimd
        def _(pool):
            def split_lo(k):
                pool.wait_ge(hi_ready[k], 1)
                pool.tensor_tensor(piece[k][3], piece[k][1], f32(piece[k][2]), ALU.subtract
                                   ).then_inc(lo_ready[k], 1)

            def inverse_root(k, g, b):
                pool.wait_ge(var_ready[k], nth(g, b))
                pool.tensor_tensor(rstd[k][:, b, :], rstd[k][:, b, :], neg_half[:], ALU.pow
                                   ).then_inc(rstd_ready[k], 1)

            def v_lo_part(n, b):
                pool.wait_ge(v_hi_ready, nth(n, b))
                pool.tensor_tensor(v_lo[:, b, :], ctx[:, b, :], f32(v_hi[:, b, :]), ALU.subtract
                                   ).then_inc(v_lo_ready, 1)

            def add_beta(n, b):
                pool.wait_ge(h_ready, nth(n, b))
                if is_first(n) and b == 0:
                    pool.wait_ge(affine_ready, 2)
                at = xs[:, PAIR * n + b, :]
                pool.tensor_tensor(at, at, beta[:], ALU.add).then_inc(x1_beta_ready, 1)

            def both(g):
                n = g + 1
                inverse_root("x", n, 0)
                v_lo_part(n, 0)
                inverse_root("x", n, 1)
                v_lo_part(n, 1)
                if is_first(g):
                    split_lo("down0")
                    split_lo("down2")
                inverse_root("x1", n, 0)
                inverse_root("x1", n, 1)
                add_beta(n, 0)
                inverse_root("y", g, 0)
                add_beta(n, 1)
                inverse_root("y", g, 1)

            pool.memset(neg_half[:], -0.5).then_inc(half_ready, 1)
            pool.memset(ident[:], 0.0).then_inc(ident_zeroed, 1)
            pool.wait_ge(ident_zeroed, 1)
            pool.affine_select(out=ident[:], in_=ident[:], compare_op=ALU.not_equal, fill=1.0, base=0,
                               pattern=[[-1, P]], channel_multiplier=1).then_inc(ident_ready, 1)
            pool.wait_ge(half_ready, 1)
            inverse_root("x", 0, 0)
            inverse_root("x", 0, 1)
            v_lo_part(0, 0)
            v_lo_part(0, 1)
            split_lo("expert")
            for c in range(KL):
                pool.wait_ge(fc1T_hi_ready, c + 1)
                pool.wait_ge(fc1T_copied, c + 1)
                pool.tensor_tensor(lat_lo[:, c, :], y[:, c, :], f32(lat_hi[:, c, :]), ALU.subtract
                                   ).then_inc(fc1T_lo_ready, 1)
            inverse_root("x1", 0, 0)
            split_lo("up0")
            inverse_root("x1", 0, 1)
            split_lo("up1")
            split_lo("up2")
            split_lo("fc2")
            add_beta(0, 0)
            add_beta(0, 1)
            both(0)
            with pool.Fori(1, GROUPS - 1) as g:
                both(g)
            g = GROUPS - 1
            for b in range(PAIR):
                inverse_root("y", g, b)


_INS = ["x", "ctx_4096", "g_xattn", "g_ffn", "L0_ffn_gate_w", "L0_ffn_up_w", "L0_ffn_down_w", "L0_ffn_fc1_w",
        "L0_ffn_fc2_w", "L0_ffn_expert_w", "L0_ffn_ln_gamma", "L0_ffn_ln_beta"]


def kernel(**inputs):
    import numpy as _np
    import concourse.bacc as _bacc
    from concourse import mybir as _mybir
    from concourse.bass_utils import run_bass_kernel_spmd as _run

    nc = _bacc.Bacc("TRN2", target_bir_lowering=False, num_devices=1)
    arrays, args = {}, []
    for name in _INS:
        a = _np.ascontiguousarray(inputs[name])
        arrays[f"in_{name}_dram"] = a
        args.append(nc.dram_tensor(f"in_{name}_dram", a.shape, _mybir.dt.from_np(a.dtype), kind="ExternalInput").ap())
    shape = inputs["x"].shape
    args.append(nc.dram_tensor("out_dram", shape, _mybir.dt.float32, kind="ExternalOutput").ap())
    flamingo_block(nc, *args)
    r = _run(nc, [arrays], core_ids=[0])
    return r.results[0]["out_dram"]
```

```python
from contextlib import ExitStack

import concourse.bass as bass
from concourse import mybir

F32 = mybir.dt.float32
F32R = mybir.dt.float32r
ALU = mybir.AluOpType
ACT = mybir.ActivationFunctionType
AX = mybir.AxisListType

P = 128
PAIR = 2
EPS = 1e-5
RING = 6
WARM_UP = 8


def flamingo_block(nc, x, ctx_in, g_xattn, g_ffn, gate_w, up_w, down_w, fc1_w, fc2_w, expert_w,
                   ln_gamma, ln_beta, out):
    BATCH, TOK, HID = x.shape
    INNER = up_w.shape[1]
    LAT = fc1_w.shape[1]
    NE = gate_w.shape[1]
    KH = HID // P
    KI = INNER // P
    KL = LAT // P
    GROUPS = BATCH // PAIR
    GT = PAIR * TOK
    UPS = KI // PAIR
    HALF = HID // 2
    SCALE = float(TOK) ** -0.5
    assert TOK == P and HID == 512 and GT * PAIR == 512 and NE == 8
    assert KL * HID == KI // 2 * GT

    def nth(n, b):
        return PAIR * n + b + 1

    def is_first(g):
        return isinstance(g, int) and g == 0

    def is_second(g):
        return isinstance(g, int) and g == 1

    def is_last(g):
        return isinstance(g, int) and g == GROUPS - 1

    stack = ExitStack()
    with stack:
        def sb(name, shape, dt=F32):
            return stack.enter_context(nc.sbuf_tensor(name, shape, dt))

        def bank(name):
            return stack.enter_context(nc.psum_tensor(name, [P, 512], F32))

        def sem(name):
            return stack.enter_context(nc.semaphore(name))

        up_bank = [bank("up_bank0"), bank("up_bank1")]
        down_bank = [bank("down_bank0"), bank("down_bank1")]
        routed_banks = stack.enter_context(nc.psum_tensor("routed_banks", [P, 2, 512], F32))
        ctx_bank = bank("ctx_bank")
        tok_bank = bank("tok_bank")

        xs = sb("xs", [P, BATCH, HID])
        ctx = sb("ctx", [P, PAIR, HID])
        v_hi = sb("v_hi", [P, PAIR, HID], F32R)
        v_lo = sb("v_lo", [P, PAIR, HID], F32R)
        ctxT = sb("ctxT", [P, PAIR, KH, 2, TOK], F32R)
        qT_hi = sb("qT_hi", [P, PAIR, KH, TOK], F32R)
        qT_lo = sb("qT_lo", [P, PAIR, KH, TOK], F32R)
        normed = sb("normed", [P, PAIR, HID])
        hT_hi = sb("hT_hi", [P, KH, GT], F32R)
        hT_lo = sb("hT_lo", [P, KH, GT], F32R)
        act2 = sb("act2", [P, 2, PAIR, GT])
        act2_hi = sb("act2_hi", [P, KI, GT], F32R)
        act2_lo = sb("act2_lo", [P, KI, GT], F32R)
        fc1T_hi, latW_hi = (act2_hi[:, at * KI // 2:(at + 1) * KI // 2, :].rearrange("p (l a) t -> p l (a t)", l=KL)
                            for at in range(2))
        fc1T_lo, latW_lo = (act2_lo[:, at * KI // 2:(at + 1) * KI // 2, :].rearrange("p (l a) t -> p l (a t)", l=KL)
                            for at in range(2))
        y = sb("y", [P, PAIR, HID])
        probs = sb("probs", [P, PAIR, TOK])
        probs_hi = sb("probs_hi", [P, PAIR, TOK], F32R)
        probs_lo = sb("probs_lo", [P, PAIR, TOK], F32R)

        raw = sb("raw", [P, RING, 1024])
        raw_expert = sb("raw_expert", [P, KL * LAT])
        up_hi = sb("up_hi", [P, UPS, KH, PAIR * P], F32R)
        up_lo = sb("up_lo", [P, UPS, KH, PAIR * P], F32R)
        down_hi = sb("down_hi", [P, KI, HID], F32R)
        down_lo = sb("down_lo", [P, KI, HID], F32R)
        W_hi = sb("W_hi", [P, KH, 2, HALF + NE], F32R)
        W_lo = sb("W_lo", [P, KH, 2, HALF + NE], F32R)
        expert_hi = sb("expert_hi", [P, KL, LAT], F32R)
        expert_lo = sb("expert_lo", [P, KL, LAT], F32R)
        fc2_hi = sb("fc2_hi", [P, KL, HID], F32R)
        fc2_lo = sb("fc2_lo", [P, KL, HID], F32R)
        gate = sb("gate", [P, KH, NE])
        gamma = sb("gamma", [P, HID])
        beta = sb("beta", [P, HID])
        gates = sb("gates", [P, 2])
        ident = sb("ident", [P, P])
        neg_half = sb("neg_half", [P, 1])

        LNS = ("x", "x1", "y")
        stats = {k: sb(f"stats_{k}", [P, PAIR, 6]) for k in LNS}
        moments = {k: sb(f"moments_{k}", [P, PAIR, 2]) for k in LNS}
        rstd = {k: sb(f"rstd_{k}", [P, PAIR, 1]) for k in LNS}
        stats_halves = sb("stats_halves", [P, 2, 6])
        neg_max = sb("neg_max", [P, PAIR, 1])
        exp_sum = sb("exp_sum", [P, PAIR, 1])
        exp_inv = sb("exp_inv", [P, PAIR, 1])
        row_max = sb("row_max", [P, PAIR, 1])
        top8 = sb("top8", [P, PAIR, 8])
        route = sb("route", [P, PAIR])

        x_loaded = [sem(f"x_loaded{b}") for b in range(PAIR)]
        ctx_loaded = [sem(f"ctx_loaded{b}") for b in range(PAIR)]
        gates_loaded = sem("gates_loaded")
        gate_loaded = sem("gate_loaded")
        affine_loaded = sem("affine_loaded")
        PIECES = ["fc1", "fc2", "up0", "up1", "up2", "up3"] + [f"down{j}" for j in range(UPS)]
        raw_loaded = {k: sem(f"{k}_loaded") for k in PIECES + ["expert"]}
        out_stored = sem("out_stored")
        waits_passed = sem("waits_passed")
        ident_zeroed = sem("ident_zeroed")
        ident_ready = sem("ident_ready")
        half_ready = sem("half_ready")
        warm_ready = sem("warm_ready")
        tanh_ready = sem("tanh_ready")
        affine_ready = sem("affine_ready")
        hi_ready = {k: sem(f"{k}_hi_ready") for k in PIECES[1:] + ["expert"]}
        lo_ready = {k: sem(f"{k}_lo_ready") for k in PIECES[1:] + ["expert"]}
        gate_hi_ready = sem("gate_hi_ready")
        gate_lo_ready = sem("gate_lo_ready")
        fc1T_made = sem("fc1T_made")
        fc1T_hi_ready = sem("fc1T_hi_ready")
        fc1T_lo_ready = sem("fc1T_lo_ready")
        latW_made = sem("latW_made")
        latW_hi_ready = sem("latW_hi_ready")
        latW_lo_ready = sem("latW_lo_ready")
        W_made = sem("W_made")
        W_hi_ready = sem("W_hi_ready")
        W_lo_ready = sem("W_lo_ready")
        stats_ready = {k: sem(f"stats_{k}_ready") for k in LNS}
        moments_ready = {k: sem(f"moments_{k}_ready") for k in LNS}
        var_ready = {k: sem(f"var_{k}_ready") for k in LNS}
        rstd_ready = {k: sem(f"rstd_{k}_ready") for k in LNS}
        q_ready = sem("q_ready")
        v_hi_ready = sem("v_hi_ready")
        v_lo_ready = sem("v_lo_ready")
        ctxT_made = sem("ctxT_made")
        ctxT_hi_ready = sem("ctxT_hi_ready")
        ctxT_lo_ready = sem("ctxT_lo_ready")
        qT_made = sem("qT_made")
        qT_hi_ready = sem("qT_hi_ready")
        qT_lo_ready = sem("qT_lo_ready")
        scores_made = sem("scores_made")
        scores_summed = sem("scores_summed")
        row_max_ready = sem("row_max_ready")
        neg_max_ready = sem("neg_max_ready")
        exp_ready = sem("exp_ready")
        exp_inv_ready = sem("exp_inv_ready")
        probs_ready = sem("probs_ready")
        probs_hi_ready = sem("probs_hi_ready")
        probs_lo_ready = sem("probs_lo_ready")
        attended = sem("attended")
        x1_ready = sem("x1_ready")
        h_ready = sem("h_ready")
        hT_made = sem("hT_made")
        hT_hi_ready = sem("hT_hi_ready")
        hT_lo_ready = sem("hT_lo_ready")
        up_made = sem("up_made")
        relu_ready = sem("relu_ready")
        square_ready = sem("square_ready")
        act2_hi_ready = sem("act2_hi_ready")
        act2_lo_ready = sem("act2_lo_ready")
        top_ready = sem("top_ready")
        route_ready = sem("route_ready")
        routed_made = sem("routed_made")
        scaled_ready = sem("scaled_ready")
        down_made = sem("down_made")
        y_ready = sem("y_ready")
        x1_beta_ready = sem("x1_beta_ready")
        y_gamma_ready = sem("y_gamma_ready")
        out_ready = sem("out_ready")
        down_half_made = sem("down_half_made")
        y_half_ready = sem("y_half_ready")
        stats_half_ready = sem("stats_half_ready")
        out_half_ready = sem("out_half_ready")

        def flat(t, *at):
            v = t[(slice(None),) + at]
            return v.rearrange("p a b -> p (a b)") if len(v.shape) == 3 else v

        def slot(k, size):
            return raw[:, PIECES.index(k) % RING, 0:size]

        piece = {
            "fc1": (fc1_w.rearrange("(k p) l -> p k l", p=P), slot("fc1", KH * LAT), None, None),
            "expert": (expert_w.rearrange("(k p) l -> p k l", p=P), raw_expert[:],
                       flat(expert_hi), flat(expert_lo)),
            "fc2": (fc2_w.rearrange("(k p) n -> p k n", p=P), slot("fc2", KL * HID), flat(fc2_hi), flat(fc2_lo)),
        }
        for j in range(UPS):
            piece[f"up{j}"] = (up_w.rearrange("(k p) i -> p k i", p=P)[:, :, j * PAIR * P:(j + 1) * PAIR * P],
                               slot(f"up{j}", KH * PAIR * P), flat(up_hi, j), flat(up_lo, j))
            piece[f"down{j}"] = (down_w.rearrange("(k p) n -> p k n", p=P)[:, PAIR * j:PAIR * (j + 1), :],
                                 slot(f"down{j}", PAIR * HID), flat(down_hi, slice(PAIR * j, PAIR * (j + 1))),
                                 flat(down_lo, slice(PAIR * j, PAIR * (j + 1))))

        def f32(ap):
            return ap.bitcast(F32)

        def turned_ctx_bank(n, b):
            if is_second(n):
                return [tok_bank, down_bank[1]][b]
            return up_bank[0] if is_first(n) and b else ctx_bank

        def turned_q_bank(n, b):
            return up_bank[1] if is_first(n) and b else tok_bank

        def turned_h_bank(n, b):
            if is_first(n) and b == 0:
                return down_bank[0]
            return [tok_bank, ctx_bank][b]

        last_bank = [down_bank[1], down_bank[0]]

        W_bank = [routed_banks[:, 0, :], routed_banks[:, 1, :], down_bank[0][:], down_bank[1][:]]

        def W_halves(t, c):
            return t[:, c, :, 0:HALF]

        def halves(ap):
            return ap.rearrange("p (a n) -> p a n", a=2)

        def chunks(bank_of):
            return bank_of[:].rearrange("p (k t) -> p k t", k=KH)

        def half(a):
            return slice(a * HALF, (a + 1) * HALF)

        def tokens(b):
            return slice(b * TOK, (b + 1) * TOK)

        def wait_apart(engine, on, value):
            engine.wait_ge(on, value)
            engine.sem_inc(waits_passed, 1)

        block = stack.enter_context(nc.Block())

        @block.sync
        def _(sp):
            def load_x(n, b):
                if not is_first(n):
                    sp.wait_ge(stats_ready["x"], nth(n, b) - PAIR)
                sp.dma_start(xs[:, PAIR * n + b, :], x[PAIR * n + b]).then_inc(x_loaded[b], 16)

            def load_ctx(n, b):
                if not is_first(n):
                    sp.wait_ge(v_hi_ready, nth(n, b) - PAIR)
                    sp.wait_ge(v_lo_ready, nth(n, b) - PAIR)
                    sp.wait_ge(ctxT_made, nth(n, b) - PAIR)
                sp.dma_start(ctx[:, b, :], ctx_in[PAIR * n + b]).then_inc(ctx_loaded[b], 16)

            def load_piece(k):
                at = 0 if k == "expert" else PIECES.index(k)
                if at >= RING:
                    before = PIECES[at - RING]
                    if before == "fc1":
                        sp.wait_ge(fc1T_made, KL)
                    else:
                        sp.wait_ge(hi_ready[before], 1)
                        sp.wait_ge(lo_ready[before], 1)
                src, dst, _, _ = piece[k]
                sp.dma_start(dst.rearrange("p (k n) -> p k n", k=src.shape[1]), src).then_inc(raw_loaded[k], 16)

            def store(g, b):
                sp.wait_ge(out_ready, nth(g, b))
                sp.dma_start(out[PAIR * g + b], xs[:, PAIR * g + b, :]).then_inc(out_stored, 16)

            load_x(0, 0)
            load_ctx(0, 0)
            load_x(0, 1)
            load_ctx(0, 1)
            load_piece("fc1")
            for g_at, g_in in enumerate((g_xattn, g_ffn)):
                sp.dma_start(gates[:, g_at:g_at + 1], g_in.rearrange("(a d) -> a d", a=1).to_broadcast([P, 1])
                             ).then_inc(gates_loaded, 16)
            load_piece("expert")
            load_piece("fc2")
            load_piece("up0")
            for b in range(PAIR):
                load_ctx(1, b)
            load_piece("up1")
            for b in range(PAIR):
                load_x(1, b)
            sp.dma_start(gate[:], gate_w.rearrange("(k p) e -> p k e", p=P)).then_inc(gate_loaded, 16)
            load_piece("up2")
            for t, src in ((gamma, ln_gamma), (beta, ln_beta)):
                sp.dma_start(t[:], src.rearrange("(a d) -> a d", a=1).to_broadcast([P, HID])
                             ).then_inc(affine_loaded, 16)
            for k in PIECES[5:]:
                load_piece(k)
            with sp.Fori(0, GROUPS - 2) as g:
                for b in range(PAIR):
                    sp.wait_ge(stats_ready["x"], PAIR * g + b + 1 + PAIR)
                    sp.dma_start(xs[:, PAIR * g + 2 * PAIR + b, :], x[PAIR * g + 2 * PAIR + b]
                                 ).then_inc(x_loaded[b], 16)
                    load_ctx(g + 2, b)
                for b in range(PAIR):
                    store(g, b)
            for b in range(PAIR):
                store(GROUPS - 2, b)
            store(GROUPS - 1, 0)
            for a in range(2):
                sp.wait_ge(out_half_ready, a + 1)
                sp.dma_start(out[BATCH - 1][:, half(a)], xs[:, BATCH - 1, half(a)]).then_inc(out_stored, 16)
            sp.wait_ge(out_stored, 16 * (BATCH + 1))

        @block.tensor
        def _(pe):
            def product(to, parts, first, last):
                mm = None
                for at, (a_hi, a_lo, b_hi, b_lo) in enumerate(parts):
                    begins, ends = first and at == 0, last and at == len(parts) - 1
                    pe.matmul(to, a_hi, b_hi, start=begins, stop=False)
                    pe.matmul(to, a_hi, b_lo, start=False, stop=False)
                    mm = pe.matmul(to, a_lo, b_hi, start=False, stop=ends)
                return mm

            def transposed(to, src, made):
                for k in range(KH):
                    mm = pe.transpose(to[:, k * P:(k + 1) * P], src[:, k * P:(k + 1) * P], ident[:])
                mm.then_inc(made, 1)

            def keep_warm(on, free_bank, count):
                for _ in range(count):
                    pe.matmul(free_bank[:, 0:P], on, on, start=True, stop=True)

            def transpose_ctx(n, b):
                pe.wait_ge(ctx_loaded[b], 16 * (n + 1))
                if is_second(n) and b == 0:
                    pe.wait_ge(qT_lo_ready, 1)
                elif is_second(n):
                    pe.wait_ge(exp_ready, nth(n, b) - PAIR)
                elif not is_first(n):
                    pe.wait_ge(ctxT_lo_ready if b else hT_lo_ready, nth(n, b) - 1)
                transposed(turned_ctx_bank(n, b), ctx[:, b, :], ctxT_made)

            def transpose_q(n, b):
                pe.wait_ge(q_ready, nth(n, b))
                if is_second(n) and b == 0:
                    pe.wait_ge(ctxT_lo_ready, nth(n, b))
                elif not is_first(n):
                    pe.wait_ge(qT_lo_ready if b else hT_lo_ready, nth(n, b) - 1)
                transposed(turned_q_bank(n, b), normed[:, b, :], qT_made)

            def scores(n, b):
                pe.wait_ge(qT_lo_ready, nth(n, b))
                pe.wait_ge(ctxT_lo_ready, nth(n, b))
                if not isinstance(n, int) or n > 1:
                    pe.wait_ge(y_ready, nth(n, b) - 2 * PAIR)
                elif n == 1:
                    pe.wait_ge(W_lo_ready, 3 + b)
                if is_first(n):
                    product(down_bank[b][:, 0:TOK],
                            [(qT_hi[:, b, k, :], qT_lo[:, b, k, :], ctxT[:, b, k, 0, :], ctxT[:, b, k, 1, :])
                             for k in range(KH)], True, True).then_inc(scores_made, 1)
                    return
                for k in range(KH):
                    pe.matmul(down_bank[b][:, 0:2 * TOK], qT_hi[:, b, k, :],
                              ctxT[:, b, k, :, :].rearrange("p a t -> p (a t)"), start=k == 0, stop=False)
                    mm = pe.matmul(down_bank[b][:, 0:TOK], qT_lo[:, b, k, :], ctxT[:, b, k, 0, :],
                                   start=False, stop=k == KH - 1)
                mm.then_inc(scores_made, 1)

            def attend(n, b):
                pe.wait_ge(probs_lo_ready, nth(n, b))
                pe.wait_ge(v_lo_ready, nth(n, b))
                pe.wait_ge(v_hi_ready, nth(n, b))
                if b:
                    pe.wait_ge(x1_ready, nth(n, b) - 1)
                elif is_second(n):
                    pe.wait_ge(hT_lo_ready, PAIR)
                else:
                    pe.wait_ge(ctxT_lo_ready, nth(n, b) + 1)
                product(ctx_bank[:], [(probs_hi[:, b, :], probs_lo[:, b, :], v_hi[:, b, :], v_lo[:, b, :])],
                        True, True).then_inc(attended, 1)

            def transpose_h(n, b):
                pe.wait_ge(h_ready, nth(n, b))
                if b:
                    pe.wait_ge(x1_ready, nth(n, b))
                elif is_first(n):
                    pe.wait_ge(exp_ready, nth(n, b))
                else:
                    pe.wait_ge(qT_lo_ready, nth(n, b) + 1)
                transposed(turned_h_bank(n, b), normed[:, b, :], hT_made)

            def transpose_fc1(c):
                pe.wait_ge(raw_loaded["fc1"], 16)
                for k in range(KH):
                    mm = pe.transpose(routed_banks[:, c, k * P:(k + 1) * P],
                                      raw[:, 0, k * LAT + c * P:k * LAT + (c + 1) * P], ident[:])
                mm.then_inc(fc1T_made, 1)

            def fc1_expert(c):
                pe.wait_ge(fc1T_lo_ready, KL)
                pe.wait_ge(qT_lo_ready if c else ctxT_lo_ready, PAIR)
                pe.wait_ge(hi_ready["expert"], 1)
                pe.wait_ge(lo_ready["expert"], 1)
                product(up_bank[c][:],
                        [(expert_hi[:, k, c * P:(c + 1) * P], expert_lo[:, k, c * P:(c + 1) * P],
                          fc1T_hi[:, k, :], fc1T_lo[:, k, :]) for k in range(KL)], True, True
                        ).then_inc(latW_made, 1)

            def make_W(c):
                pe.wait_ge(latW_lo_ready, KL)
                pe.wait_ge(hi_ready["fc2"], 1)
                pe.wait_ge(lo_ready["fc2"], 1)
                if c == 2:
                    pe.wait_ge(hT_lo_ready, nth(0, 0))
                elif c == 3:
                    pe.wait_ge(ctxT_lo_ready, nth(1, 1))
                product(W_bank[c],
                        [(latW_hi[:, k, c * P:(c + 1) * P], latW_lo[:, k, c * P:(c + 1) * P],
                          fc2_hi[:, k, :], fc2_lo[:, k, :]) for k in range(KL)], True, True
                        ).then_inc(W_made, 1)

            def up(g, j):
                if j == 0:
                    pe.wait_ge(hT_lo_ready, nth(g, PAIR - 1))
                if not is_first(g) or j >= 2:
                    pe.wait_ge(relu_ready, UPS * g + j + 1 - 2)
                elif j == 0:
                    pe.wait_ge(latW_lo_ready, KL)
                pe.wait_ge(hi_ready[f"up{j}"], 1)
                pe.wait_ge(lo_ready[f"up{j}"], 1)
                for c in range(PAIR):
                    mm = product(up_bank[j % 2][:, c * GT:(c + 1) * GT],
                                 [(up_hi[:, j, k, c * P:(c + 1) * P], up_lo[:, j, k, c * P:(c + 1) * P],
                                   hT_hi[:, k, :], hT_lo[:, k, :]) for k in range(KH)], True, True)
                mm.then_inc(up_made, 1)

            def routed(g, b):
                if b == 0:
                    pe.wait_ge(W_lo_ready, KH)
                    pe.wait_ge(gate_lo_ready, 1)
                if b or not is_first(g):
                    pe.wait_ge(scaled_ready, nth(g, b) - 1)
                for a, size in enumerate((HALF + NE, HALF)):
                    mm = product(routed_banks[:, a, 0:size],
                                 [(hT_hi[:, k, tokens(b)], hT_lo[:, k, tokens(b)],
                                   W_hi[:, k, a, 0:size], W_lo[:, k, a, 0:size]) for k in range(KH)], True, True)
                mm.then_inc(routed_made, 1)

            def down(g, b, j):
                if j == 0 and not is_last(g):
                    pe.wait_ge(scores_summed, nth(g, b))
                elif j == 0:
                    pe.wait_ge(y_ready, nth(g, b) - PAIR)
                pe.wait_ge(act2_lo_ready, UPS * g + j + 1)
                pe.wait_ge(hi_ready[f"down{j}"], 1)
                pe.wait_ge(lo_ready[f"down{j}"], 1)
                mm = product(down_bank[b][:],
                             [(act2_hi[:, i, tokens(b)], act2_lo[:, i, tokens(b)],
                               down_hi[:, i, :], down_lo[:, i, :]) for i in range(PAIR * j, PAIR * (j + 1))],
                             j == 0, j == UPS - 1)
                if j == UPS - 1:
                    mm.then_inc(down_made, 1)

            def both(g):
                n = g + 1
                up(g, 0)
                if not is_first(g):
                    transpose_ctx(n, 0)
                up(g, 1)
                if not is_first(g):
                    transpose_ctx(n, 1)
                up(g, 2)
                routed(g, 0)
                transpose_q(n, 0)
                up(g, 3)
                transpose_q(n, 1)
                routed(g, 1)
                scores(n, 0)
                scores(n, 1)
                down(g, 0, 0)
                down(g, 0, 1)
                attend(n, 0)
                down(g, 0, 2)
                attend(n, 1)
                down(g, 0, 3)
                down(g, 1, 0)
                transpose_h(n, 0)
                down(g, 1, 1)
                transpose_h(n, 1)
                down(g, 1, 2)
                down(g, 1, 3)

            pe.wait_ge(warm_ready, 1)
            keep_warm(probs[:, 0, :], up_bank[0], WARM_UP)
            pe.wait_ge(ident_ready, 1)
            transpose_ctx(0, 0)
            transpose_q(0, 0)
            transpose_ctx(0, 1)
            transpose_fc1(0)
            transpose_q(0, 1)
            scores(0, 0)
            transpose_fc1(1)
            scores(0, 1)
            transpose_ctx(1, 0)
            attend(0, 0)
            fc1_expert(0)
            fc1_expert(1)
            attend(0, 1)
            transpose_ctx(1, 1)
            transpose_h(0, 0)
            make_W(0)
            make_W(1)
            transpose_h(0, 1)
            make_W(2)
            make_W(3)
            both(0)
            with pe.Fori(1, GROUPS - 1) as g:
                both(g)
            g = GROUPS - 1
            for j in range(UPS):
                up(g, j)
            routed(g, 0)
            for j in range(UPS):
                down(g, 0, j)
            routed(g, 1)
            for a in range(2):
                pe.wait_ge(y_ready, BATCH - (1 if a else PAIR))
                product(last_bank[a][:, 0:HALF],
                        [(act2_hi[:, i, tokens(1)], act2_lo[:, i, tokens(1)],
                          down_hi[:, i, half(a)], down_lo[:, i, half(a)]) for i in range(KI)], True, True
                        ).then_inc(down_half_made, 1)

        @block.scalar
        def _(act):
            def copied(to, src, ready):
                act.activation(to, src, ACT.Identity).then_inc(ready, 1)

            def split_hi(k):
                act.wait_ge(raw_loaded[k], 16)
                copied(piece[k][2], piece[k][1], hi_ready[k])

            def ctxT_hi_part(n, b):
                act.wait_ge(ctxT_made, nth(n, b))
                if not is_first(n):
                    act.wait_ge(scores_made, nth(n, b) - PAIR)
                copied(ctxT[:, b, :, 0, :], chunks(turned_ctx_bank(n, b)), ctxT_hi_ready)

            def qT_hi_part(n, b):
                act.wait_ge(qT_made, nth(n, b))
                if not is_first(n):
                    act.wait_ge(scores_made, nth(n, b) - PAIR)
                copied(flat(qT_hi, b), turned_q_bank(n, b)[:], qT_hi_ready)

            def v_hi_part(n, b):
                act.wait_ge(ctx_loaded[b], 16 * (n + 1))
                if not is_first(n):
                    act.wait_ge(attended, nth(n, b) - PAIR)
                copied(v_hi[:, b, :], ctx[:, b, :], v_hi_ready)

            def exponentials(n, b):
                act.wait_ge(neg_max_ready, nth(n, b))
                src = down_bank[b][:, 0:TOK] if is_first(n) else probs[:, b, :]
                act.activation(probs[:, b, :], src, ACT.Exp, bias=neg_max[:, b, :], scale=SCALE,
                               accum_out=exp_sum[:, b, :]).then_inc(exp_ready, 1)

            def hT_hi_part(n, b):
                act.wait_ge(hT_made, nth(n, b))
                if not is_first(n):
                    act.wait_ge(routed_made, nth(n, b) - PAIR)
                copied(hT_hi[:, :, tokens(b)], chunks(turned_h_bank(n, b)),
                       hT_hi_ready)

            def relu(g, j):
                at = act2[:, j % 2, :, :].rearrange("p a t -> p (a t)")
                act.wait_ge(up_made, UPS * g + j + 1)
                if not is_first(g) or j >= 2:
                    act.wait_ge(act2_lo_ready, UPS * g + j + 1 - 2)
                act.activation(at, up_bank[j % 2][:], ACT.Relu).then_inc(relu_ready, 1)

            def square(g, j):
                at = act2[:, j % 2, :, :].rearrange("p a t -> p (a t)")
                act.wait_ge(relu_ready, UPS * g + j + 1)
                if j == 0 and not is_first(g):
                    act.wait_ge(down_made, PAIR * g)
                act.activation(flat(act2_hi, slice(PAIR * j, PAIR * (j + 1))), at, ACT.Square
                               ).then_inc(act2_hi_ready, 1)
                act.wait_ge(act2_hi_ready, UPS * g + j + 1)
                act.activation(at, at, ACT.Square).then_inc(square_ready, 1)

            def scaled(g, b):
                act.wait_ge(routed_made, nth(g, b))
                act.wait_ge(route_ready, nth(g, b))
                if not is_first(g):
                    act.wait_ge(out_ready, nth(g, b) - PAIR)
                act.activation(halves(y[:, b, :]), routed_banks[:, :, 0:HALF], ACT.Identity, scale=route[:, b:b + 1]
                               ).then_inc(scaled_ready, 1)

            def fc1T_hi_part(c):
                act.wait_ge(fc1T_made, c + 1)
                copied(fc1T_hi[:, c, :], routed_banks[:, c, :], fc1T_hi_ready)

            def latW_hi_part(c):
                act.wait_ge(latW_made, c + 1)
                copied(latW_hi[:, c, :], up_bank[c][:], latW_hi_ready)

            def scale_affine():
                act.wait_ge(affine_loaded, 32)
                act.wait_ge(tanh_ready, 1)
                for t in (gamma, beta):
                    act.activation(t[:], t[:], ACT.Identity, scale=gates[:, 1:2]).then_inc(affine_ready, 1)

            def both(g):
                n = g + 1
                relu(g, 0)
                if not is_first(g):
                    ctxT_hi_part(n, 0)
                square(g, 0)
                if is_first(g):
                    split_hi("down0")
                else:
                    v_hi_part(n, 0)
                relu(g, 1)
                if not is_first(g):
                    ctxT_hi_part(n, 1)
                square(g, 1)
                if is_first(g):
                    split_hi("down1")
                else:
                    v_hi_part(n, 1)
                relu(g, 2)
                square(g, 2)
                if is_first(g):
                    split_hi("down2")
                scaled(g, 0)
                qT_hi_part(n, 0)
                relu(g, 3)
                square(g, 3)
                qT_hi_part(n, 1)
                if is_first(g):
                    split_hi("down3")
                scaled(g, 1)
                exponentials(n, 0)
                exponentials(n, 1)
                if is_first(g):
                    scale_affine()
                hT_hi_part(n, 0)
                hT_hi_part(n, 1)

            ctxT_hi_part(0, 0)
            v_hi_part(0, 0)
            qT_hi_part(0, 0)
            ctxT_hi_part(0, 1)
            v_hi_part(0, 1)
            qT_hi_part(0, 1)
            fc1T_hi_part(0)
            act.wait_ge(gates_loaded, 32)
            act.activation(gates[:], gates[:], ACT.Tanh).then_inc(tanh_ready, 1)
            split_hi("expert")
            exponentials(0, 0)
            fc1T_hi_part(1)
            split_hi("fc2")
            exponentials(0, 1)
            split_hi("up0")
            latW_hi_part(0)
            ctxT_hi_part(1, 0)
            latW_hi_part(1)
            split_hi("up1")
            hT_hi_part(0, 0)
            ctxT_hi_part(1, 1)
            split_hi("up2")
            hT_hi_part(0, 1)
            v_hi_part(1, 0)
            for c in range(KH):
                act.wait_ge(W_made, c + 1)
                copied(W_halves(W_hi, c), halves(W_bank[c]), W_hi_ready)
            split_hi("up3")
            v_hi_part(1, 1)
            both(0)
            with act.Fori(1, GROUPS - 1) as g:
                both(g)
            g = GROUPS - 1
            for j in range(UPS):
                relu(g, j)
                square(g, j)
            for b in range(PAIR):
                scaled(g, b)

        @block.vector
        def _(dve):
            def rest(to, whole, hi, ready):
                dve.tensor_tensor(to, whole, f32(hi), ALU.subtract).then_inc(ready, 1)

            def layernorm_stats(k, src, g, b):
                dve.bn_stats(stats[k][:, b, :], src).then_inc(stats_ready[k], 1)
                wait_apart(dve, stats_ready[k], nth(g, b))
                dve.bn_aggr(moments[k][:, b, :], stats[k][:, b, :]).then_inc(moments_ready[k], 1)
                dve.wait_ge(moments_ready[k], nth(g, b))
                dve.tensor_scalar(rstd[k][:, b, :], moments[k][:, b, 1:2], EPS, None, ALU.add
                                  ).then_inc(var_ready[k], 1)

            def q_stats(n, b):
                wait_apart(dve, x_loaded[b], 16 * (n + 1))
                layernorm_stats("x", xs[:, PAIR * n + b, :], n, b)

            def make_q(n, b):
                dve.wait_ge(rstd_ready["x"], nth(n, b))
                if not is_first(n):
                    dve.wait_ge(hT_made, nth(n, b) - PAIR)
                dve.tensor_scalar(normed[:, b, :], xs[:, PAIR * n + b, :], moments["x"][:, b, 0:1],
                                  rstd["x"][:, b, :], ALU.subtract, ALU.mult).then_inc(q_ready, 1)

            def ctxT_lo_part(n, b):
                dve.wait_ge(ctxT_hi_ready, nth(n, b))
                rest(ctxT[:, b, :, 1, :], chunks(turned_ctx_bank(n, b)), ctxT[:, b, :, 0, :], ctxT_lo_ready)

            def qT_lo_part(n, b):
                dve.wait_ge(qT_hi_ready, nth(n, b))
                rest(flat(qT_lo, b), turned_q_bank(n, b)[:], flat(qT_hi, b), qT_lo_ready)

            def rows_max(n, b):
                dve.wait_ge(scores_made, nth(n, b))
                src = down_bank[b][:, 0:TOK]
                if not is_first(n):
                    dve.wait_ge(probs_lo_ready, nth(n, b) - PAIR)
                    dve.tensor_reduce(probs[:, b, :], down_bank[b][:, 0:2 * TOK].rearrange("p (a t) -> p t a", a=2),
                                      AX.X, ALU.add).then_inc(scores_summed, 1)
                    dve.wait_ge(scores_summed, nth(n, b) - PAIR)
                    src = probs[:, b, :]
                dve.tensor_reduce(row_max[:, b, :], src, AX.X, ALU.max).then_inc(row_max_ready, 1)

            def negate_max(n, b):
                dve.wait_ge(row_max_ready, nth(n, b))
                dve.tensor_scalar(neg_max[:, b, :], row_max[:, b, :], -SCALE, None, ALU.mult
                                  ).then_inc(neg_max_ready, 1)

            def score_max(n, b):
                rows_max(n, b)
                negate_max(n, b)

            def make_probs_hi(n, b):
                dve.wait_ge(exp_ready, nth(n, b))
                dve.reciprocal(exp_inv[:, b, :], exp_sum[:, b, :]).then_inc(exp_inv_ready, 1)
                dve.wait_ge(exp_inv_ready, nth(n, b))
                if is_first(n):
                    dve.wait_ge(tanh_ready, 1)
                dve.tensor_scalar(probs[:, b, :], probs[:, b, :], exp_inv[:, b, :], gates[:, 0:1],
                                  ALU.mult, ALU.mult).then_inc(probs_ready, 1)
                dve.wait_ge(probs_ready, nth(n, b))
                if not is_first(n):
                    dve.wait_ge(attended, nth(n, b) - PAIR)
                dve.tensor_copy(probs_hi[:, b, :], probs[:, b, :]).then_inc(probs_hi_ready, 1)

            def make_probs_lo(n, b):
                dve.wait_ge(probs_hi_ready, nth(n, b))
                rest(probs_lo[:, b, :], probs[:, b, :], probs_hi[:, b, :], probs_lo_ready)

            def make_probs(n, b):
                make_probs_hi(n, b)
                make_probs_lo(n, b)

            def add_attended(n, b):
                at = xs[:, PAIR * n + b, :]
                dve.wait_ge(attended, nth(n, b))
                dve.tensor_tensor(at, at, ctx_bank[:], ALU.add).then_inc(x1_ready, 1)

            def x1_stats(n, b):
                wait_apart(dve, x1_ready, nth(n, b))
                layernorm_stats("x1", xs[:, PAIR * n + b, :], n, b)

            def make_x1(n, b):
                add_attended(n, b)
                x1_stats(n, b)

            def make_h(n, b):
                dve.wait_ge(rstd_ready["x1"], nth(n, b))
                dve.wait_ge(qT_made, nth(n, b))
                dve.tensor_scalar(normed[:, b, :], xs[:, PAIR * n + b, :], moments["x1"][:, b, 0:1],
                                  rstd["x1"][:, b, :], ALU.subtract, ALU.mult).then_inc(h_ready, 1)

            def hT_lo_part(n, b):
                dve.wait_ge(hT_hi_ready, nth(n, b))
                rest(hT_lo[:, :, tokens(b)], chunks(turned_h_bank(n, b)),
                     hT_hi[:, :, tokens(b)], hT_lo_ready)

            def square_lo_part(g, j):
                src = act2[:, j % 2, :, :].rearrange("p a t -> p (a t)")
                hi = flat(act2_hi, slice(PAIR * j, PAIR * (j + 1)))
                lo = flat(act2_lo, slice(PAIR * j, PAIR * (j + 1)))
                dve.wait_ge(square_ready, UPS * g + j + 1)
                if j == 0 and not is_first(g):
                    dve.wait_ge(down_made, PAIR * g)
                rest(lo, src, hi, act2_lo_ready)

            def router_weight(g, b):
                wait_apart(dve, routed_made, nth(g, b))
                dve.max(top8[:, b, :], routed_banks[:, 0, HALF:HALF + NE]).then_inc(top_ready, 1)
                dve.wait_ge(top_ready, nth(g, b))
                if not is_first(g):
                    dve.wait_ge(scaled_ready, nth(g, b) - PAIR)
                dve.tensor_reduce(route[:, b:b + 1], top8[:, b, 0:2], AX.X, ALU.add).then_inc(route_ready, 1)

            def add_down(g, b):
                dve.wait_ge(down_made, nth(g, b))
                dve.wait_ge(scaled_ready, nth(g, b))
                dve.tensor_tensor(y[:, b, :], y[:, b, :], down_bank[b][:], ALU.add).then_inc(y_ready, 1)

            def y_stats(g, b):
                wait_apart(dve, y_ready, nth(g, b))
                layernorm_stats("y", y[:, b, :], g, b)

            def make_out(g, b):
                at = xs[:, PAIR * g + b, :]
                if is_first(g) and b == 0:
                    dve.wait_ge(affine_ready, 2)
                dve.scalar_tensor_tensor(out=y[:, b, :], in0=y[:, b, :], scalar=moments["y"][:, b, 0:1],
                                         in1=gamma[:], op0=ALU.subtract, op1=ALU.mult).then_inc(y_gamma_ready, 1)
                dve.wait_ge(y_gamma_ready, nth(g, b))
                dve.wait_ge(x1_beta_ready, nth(g, b))
                dve.wait_ge(rstd_ready["y"], nth(g, b))
                dve.scalar_tensor_tensor(out=at, in0=y[:, b, :], scalar=rstd["y"][:, b, :], in1=at,
                                         op0=ALU.mult, op1=ALU.add).then_inc(out_ready, 1)

            def fc1T_lo_part(c):
                dve.wait_ge(fc1T_hi_ready, c + 1)
                rest(fc1T_lo[:, c, :], routed_banks[:, c, :], fc1T_hi[:, c, :], fc1T_lo_ready)

            def latW_lo_part(c):
                dve.wait_ge(latW_hi_ready, c + 1)
                rest(latW_lo[:, c, :], up_bank[c][:], latW_hi[:, c, :], latW_lo_ready)

            def both(g):
                n = g + 1
                if not is_first(g):
                    ctxT_lo_part(n, 0)
                square_lo_part(g, 0)
                if not is_first(g):
                    q_stats(n, 0)
                    ctxT_lo_part(n, 1)
                make_q(n, 0)
                square_lo_part(g, 1)
                if not is_first(g):
                    q_stats(n, 1)
                make_q(n, 1)
                square_lo_part(g, 2)
                router_weight(g, 0)
                qT_lo_part(n, 0)
                square_lo_part(g, 3)
                qT_lo_part(n, 1)
                router_weight(g, 1)
                score_max(n, 0)
                score_max(n, 1)
                make_probs(n, 0)
                make_probs(n, 1)
                make_x1(n, 0)
                add_attended(n, 1)
                make_h(n, 0)
                x1_stats(n, 1)
                add_down(g, 0)
                make_h(n, 1)
                y_stats(g, 0)
                hT_lo_part(n, 0)
                hT_lo_part(n, 1)
                make_out(g, 0)
                add_down(g, 1)
                y_stats(g, 1)
                make_out(g, 1)

            dve.memset(probs[:, 0, :], 0.0).then_inc(warm_ready, 1)
            q_stats(0, 0)
            make_q(0, 0)
            q_stats(0, 1)
            ctxT_lo_part(0, 0)
            make_q(0, 1)
            qT_lo_part(0, 0)
            ctxT_lo_part(0, 1)
            qT_lo_part(0, 1)
            score_max(0, 0)
            fc1T_lo_part(0)
            make_probs_hi(0, 0)
            rows_max(0, 1)
            make_probs_lo(0, 0)
            negate_max(0, 1)
            fc1T_lo_part(1)
            make_probs(0, 1)
            make_x1(0, 0)
            latW_lo_part(0)
            make_h(0, 0)
            latW_lo_part(1)
            add_attended(0, 1)
            x1_stats(0, 1)
            hT_lo_part(0, 0)
            make_h(0, 1)
            ctxT_lo_part(1, 0)
            ctxT_lo_part(1, 1)
            hT_lo_part(0, 1)
            q_stats(1, 0)
            q_stats(1, 1)
            for c in range(KH):
                dve.wait_ge(W_hi_ready, c + 1)
                rest(W_halves(W_lo, c), halves(W_bank[c]), W_halves(W_hi, c), W_lo_ready)
            dve.wait_ge(gate_loaded, 16)
            dve.tensor_copy(W_hi[:, :, 0, HALF:HALF + NE], gate[:]).then_inc(gate_hi_ready, 1)
            dve.wait_ge(gate_hi_ready, 1)
            rest(W_lo[:, :, 0, HALF:HALF + NE], gate[:], W_hi[:, :, 0, HALF:HALF + NE], gate_lo_ready)
            both(0)
            with dve.Fori(1, GROUPS - 1) as g:
                both(g)
            g = GROUPS - 1
            for j in range(UPS):
                square_lo_part(g, j)
            router_weight(g, 0)
            add_down(g, 0)
            y_stats(g, 0)
            make_out(g, 0)
            router_weight(g, 1)
            at = PAIR - 1
            dve.wait_ge(scaled_ready, BATCH)
            for a in range(2):
                dve.wait_ge(down_half_made, a + 1)
                dve.tensor_tensor(y[:, at, half(a)], y[:, at, half(a)], last_bank[a][:, 0:HALF], ALU.add
                                  ).then_inc(y_half_ready, 1)
                wait_apart(dve, y_half_ready, a + 1)
                dve.bn_stats(stats_halves[:, a, :], y[:, at, half(a)]).then_inc(stats_half_ready, 1)
            wait_apart(dve, stats_half_ready, 2)
            dve.bn_aggr(moments["y"][:, at, :], stats_halves[:].rearrange("p a s -> p (a s)")
                        ).then_inc(moments_ready["y"], 1)
            dve.wait_ge(moments_ready["y"], BATCH)
            dve.tensor_scalar(rstd["y"][:, at, :], moments["y"][:, at, 1:2], EPS, None, ALU.add
                              ).then_inc(var_ready["y"], 1)
            dve.scalar_tensor_tensor(out=y[:, at, :], in0=y[:, at, :], scalar=moments["y"][:, at, 0:1],
                                     in1=gamma[:], op0=ALU.subtract, op1=ALU.mult).then_inc(y_gamma_ready, 1)
            dve.wait_ge(y_gamma_ready, BATCH)
            dve.wait_ge(x1_beta_ready, BATCH)
            dve.wait_ge(rstd_ready["y"], BATCH)
            for a in range(2):
                whole = xs[:, BATCH - 1, half(a)]
                dve.scalar_tensor_tensor(out=whole, in0=y[:, at, half(a)], scalar=rstd["y"][:, at, :], in1=whole,
                                         op0=ALU.mult, op1=ALU.add).then_inc(out_half_ready, 1)

        @block.gpsimd
        def _(pool):
            def split_lo(k):
                pool.wait_ge(hi_ready[k], 1)
                pool.tensor_tensor(piece[k][3], piece[k][1], f32(piece[k][2]), ALU.subtract
                                   ).then_inc(lo_ready[k], 1)

            def inverse_root(k, g, b):
                pool.wait_ge(var_ready[k], nth(g, b))
                pool.tensor_tensor(rstd[k][:, b, :], rstd[k][:, b, :], neg_half[:], ALU.pow
                                   ).then_inc(rstd_ready[k], 1)

            def v_lo_part(n, b):
                pool.wait_ge(v_hi_ready, nth(n, b))
                pool.tensor_tensor(v_lo[:, b, :], ctx[:, b, :], f32(v_hi[:, b, :]), ALU.subtract
                                   ).then_inc(v_lo_ready, 1)

            def add_beta(n, b):
                pool.wait_ge(h_ready, nth(n, b))
                if is_first(n) and b == 0:
                    pool.wait_ge(affine_ready, 2)
                at = xs[:, PAIR * n + b, :]
                pool.tensor_tensor(at, at, beta[:], ALU.add).then_inc(x1_beta_ready, 1)

            def both(g):
                n = g + 1
                if not is_first(g):
                    v_lo_part(n, 0)
                    inverse_root("x", n, 0)
                    inverse_root("x", n, 1)
                    v_lo_part(n, 1)
                inverse_root("x1", n, 0)
                inverse_root("x1", n, 1)
                add_beta(n, 0)
                inverse_root("y", g, 0)
                add_beta(n, 1)
                inverse_root("y", g, 1)

            pool.memset(neg_half[:], -0.5).then_inc(half_ready, 1)
            pool.memset(ident[:], 0.0).then_inc(ident_zeroed, 1)
            pool.wait_ge(ident_zeroed, 1)
            pool.affine_select(out=ident[:], in_=ident[:], compare_op=ALU.not_equal, fill=1.0, base=0,
                               pattern=[[-1, P]], channel_multiplier=1).then_inc(ident_ready, 1)
            pool.wait_ge(half_ready, 1)
            inverse_root("x", 0, 0)
            inverse_root("x", 0, 1)
            v_lo_part(0, 0)
            v_lo_part(0, 1)
            split_lo("expert")
            split_lo("fc2")
            inverse_root("x1", 0, 0)
            split_lo("up0")
            inverse_root("x1", 0, 1)
            split_lo("up1")
            split_lo("up2")
            inverse_root("x", 1, 0)
            inverse_root("x", 1, 1)
            split_lo("up3")
            for j in range(UPS - 1):
                split_lo(f"down{j}")
            v_lo_part(1, 0)
            v_lo_part(1, 1)
            split_lo(f"down{UPS - 1}")
            add_beta(0, 0)
            add_beta(0, 1)
            both(0)
            with pool.Fori(1, GROUPS - 1) as g:
                both(g)
            g = GROUPS - 1
            for b in range(PAIR):
                inverse_root("y", g, b)


_INS = ["x", "ctx_4096", "g_xattn", "g_ffn", "L0_ffn_gate_w", "L0_ffn_up_w", "L0_ffn_down_w", "L0_ffn_fc1_w",
        "L0_ffn_fc2_w", "L0_ffn_expert_w", "L0_ffn_ln_gamma", "L0_ffn_ln_beta"]


def kernel(**inputs):
    import numpy as _np
    import concourse.bacc as _bacc
    from concourse import mybir as _mybir
    from concourse.bass_utils import run_bass_kernel_spmd as _run

    nc = _bacc.Bacc("TRN2", target_bir_lowering=False, num_devices=1)
    arrays, args = {}, []
    for name in _INS:
        a = _np.ascontiguousarray(inputs[name])
        arrays[f"in_{name}_dram"] = a
        args.append(nc.dram_tensor(f"in_{name}_dram", a.shape, _mybir.dt.from_np(a.dtype), kind="ExternalInput").ap())
    shape = inputs["x"].shape
    args.append(nc.dram_tensor("out_dram", shape, _mybir.dt.float32, kind="ExternalOutput").ap())
    flamingo_block(nc, *args)
    r = _run(nc, [arrays], core_ids=[0])
    return r.results[0]["out_dram"]
```
